# Optimizing a Trainium2 kernel written in Bass

```python
import numpy as np
import jax
import jax.numpy as jnp

def _softmax(x, axis=-1):
    return jax.nn.softmax(x, axis=axis)

def _gelu(x):
    return jax.nn.gelu(x, approximate=True)

def _silu(x):
    return jax.nn.silu(x)

def _sigmoid(x):
    return jax.nn.sigmoid(x)

def _layernorm(x, axis=-1, eps=1e-05):
    m = jnp.mean(x, axis=axis, keepdims=True)
    v = jnp.var(x, axis=axis, keepdims=True)
    return (x - m) / jnp.sqrt(v + eps)

def _scatter_add(tgt, idx, src, axis=0):
    return tgt.at[idx].add(src)

def _segment_sum(src, seg, n):
    return jax.ops.segment_sum(src, seg, n)
kernel_name = 'mk_adaln_ffn_d1_seqx_r2_9ae607'

def setup_inputs(seed: int=0):
    np.random.seed(seed)
    _w = jnp.asarray

    def _rec_inputs():
        import jax
        import jax.numpy as jnp
        _rk = jax.random.key(seed)
        x = -0.0003929 + 0.9999 * jax.random.normal(jax.random.fold_in(_rk, 1), (64, 128, 512), jnp.float32)
        _lenS = 128 - jax.random.randint(jax.random.fold_in(_rk, 7), (64,), 0, max(1, 128 // 4) + 1, jnp.int32)
        _lenS2 = 128 - jax.random.randint(jax.random.fold_in(_rk, 8), (64,), 0, max(1, 128 // 4) + 1, jnp.int32)
        itok_B_0_2 = jax.random.randint(jax.random.fold_in(_rk, 11), (64,), 0, 3, jnp.int32)
        return (x, itok_B_0_2)
    x, itok_B_0_2 = _rec_inputs()

    def _L0_cond_setup():
        import jax, jax.numpy as jnp
        import numpy as np
        NEG_INF = -1e+30
        key = jax.random.key(seed)
        k1, k2, k3, k4, k5 = jax.random.split(key, 5)
        B, S, D, A = (16, 512, 512, 128)
        hidden = jax.random.normal(k1, (B, S, D), dtype=jnp.float32)
        W1 = jax.random.normal(k2, (D, A), dtype=jnp.float32) / np.sqrt(D)
        b1 = jax.random.normal(k3, (A,), dtype=jnp.float32) * 0.01
        v = jax.random.normal(k4, (A,), dtype=jnp.float32) / np.sqrt(A)
        prompt_type_ids = jax.random.randint(k5, (B,), 0, 3, dtype=jnp.int32)
        return {'hidden': hidden, 'W1': W1, 'b1': b1, 'v': v, 'prompt_type_ids': prompt_type_ids}
    _L0_cond_all = _L0_cond_setup()
    _L0_cond_in = {k: v for k, v in _L0_cond_all.items() if k in ('W1', 'b1', 'v')}
    del _L0_cond_all

    def _L0_ffn_setup():
        import jax, jax.numpy as jnp
        import numpy as np
        B, T, C, D = (2, 2048, 512, 128)
        E = 8
        MIN_E = 2
        EPS = 1e-12
        NEG = -1000000000.0

        def _xavier(key, shape, fan_in, fan_out):
            bound = (6.0 / (fan_in + fan_out)) ** 0.5
            return jax.random.uniform(key, shape, jnp.float32, -bound, bound)

        def _forward(hidden_states, sim_matrix, gates, q_proj, k_proj, v_proj, o_proj):
            b, t, c = hidden_states.shape
            x = hidden_states.reshape(b * t, c)
            xn = x / jnp.maximum(jnp.linalg.norm(x, axis=-1, keepdims=True), EPS)
            sn = sim_matrix / jnp.maximum(jnp.linalg.norm(sim_matrix, axis=0, keepdims=True), EPS)
            logits = xn @ sn - jax.nn.sigmoid(gates)
            gated = jax.nn.relu(logits)
            mask = (gated > 0).astype(logits.dtype)
            inactive = jnp.sum(mask, axis=1) == 0
            top_idx = jax.lax.top_k(logits, MIN_E)[1]
            n = mask.shape[0]
            fb = jnp.zeros_like(mask).at[jnp.arange(n)[:, None], top_idx].set(1.0)
            mask = jnp.where(inactive[:, None] & (fb > 0), 1.0, mask)
            masked_logits = jnp.where(mask > 0, gated, NEG)
            routing_weights = jax.nn.softmax(masked_logits, axis=-1)
            m = jax.lax.stop_gradient(mask)
            q = jnp.einsum('tc,ecd,te->td', x, q_proj, m)
            k = jnp.einsum('tc,ecd,te->td', x, k_proj, m)
            v = jnp.einsum('tc,ecd,te->td', x, v_proj, m)
            qh = q.reshape(b, t, D)
            kh = k.reshape(b, t, D)
            vh = v.reshape(b, t, D)
            scores = jnp.einsum('bqd,bkd->bqk', qh, kh) / jnp.sqrt(jnp.asarray(D, qh.dtype))
            causal = jnp.tril(jnp.ones((t, t), bool))
            scores = jnp.where(causal, scores, jnp.finfo(scores.dtype).min)
            attn = jax.nn.softmax(scores, axis=-1)
            attn_out = jnp.einsum('bqk,bkd->bqd', attn, vh).reshape(b * t, D)
            final = jnp.einsum('td,edc,te->tc', attn_out, o_proj, m * routing_weights)
            return final.reshape(b, t, c)
        key = jax.random.key(seed)
        k = jax.random.split(key, 6)
        hidden_states = jax.random.normal(k[0], (B, T, C), jnp.float32)
        sim_matrix = jax.random.normal(k[1], (C, E), jnp.float32)
        gates = jnp.zeros((E,), jnp.float32)
        q_proj = _xavier(k[2], (E, C, D), C, D)
        k_proj = _xavier(k[3], (E, C, D), C, D)
        v_proj = _xavier(k[4], (E, C, D), C, D)
        o_proj = _xavier(k[5], (E, D, C), D, C)
        return dict(hidden_states=hidden_states, sim_matrix=sim_matrix, gates=gates, q_proj=q_proj, k_proj=k_proj, v_proj=v_proj, o_proj=o_proj)
    _L0_ffn_all = _L0_ffn_setup()
    _L0_ffn_in = {k: v for k, v in _L0_ffn_all.items() if k in ('sim_matrix', 'gates', 'q_proj', 'k_proj', 'v_proj', 'o_proj')}
    del _L0_ffn_all
    return {'x': x, 'itok_B_0_2': itok_B_0_2, 'L0_cond_W1': _L0_cond_in['W1'], 'L0_cond_b1': _L0_cond_in['b1'], 'L0_cond_v': _L0_cond_in['v'], 'L0_ffn_sim_matrix': _L0_ffn_in['sim_matrix'], 'L0_ffn_gates': _L0_ffn_in['gates'], 'L0_ffn_q_proj': _L0_ffn_in['q_proj'], 'L0_ffn_k_proj': _L0_ffn_in['k_proj'], 'L0_ffn_v_proj': _L0_ffn_in['v_proj'], 'L0_ffn_o_proj': _L0_ffn_in['o_proj']}

def reference(x, itok_B_0_2, L0_cond_W1, L0_cond_b1, L0_cond_v, L0_ffn_sim_matrix, L0_ffn_gates, L0_ffn_q_proj, L0_ffn_k_proj, L0_ffn_v_proj, L0_ffn_o_proj):
    import jax
    import jax.numpy as jnp

    def _L0_cond_ref(hidden, W1, b1, v, prompt_type_ids):
        import jax, jax.numpy as jnp
        import numpy as np
        NEG_INF = -1e+30
        B, S, D = hidden.shape
        attn_in = jnp.tanh(jnp.einsum('bsd,da->bsa', hidden, W1) + b1)
        scores = jnp.einsum('bsa,a->bs', attn_in, v)
        idx = jnp.arange(S)
        j = idx[:, None]
        l = idx[None, :]
        prefix_m = l <= j
        postfix_m = l >= j
        cloze_m = l != j
        pt = prompt_type_ids[:, None, None]
        mask = jnp.where(pt == 0, prefix_m[None], jnp.where(pt == 1, postfix_m[None], cloze_m[None]))
        masked_scores = jnp.where(mask, scores[:, None, :], NEG_INF)
        p = jax.nn.softmax(masked_scores, axis=-1)
        cnt = jnp.sum(mask, axis=-1).astype(hidden.dtype)
        pooled = jnp.einsum('bjl,bld->bjd', p, hidden) / cnt[..., None]
        return pooled

    def _L0_ffn_ref(hidden_states, sim_matrix, gates, q_proj, k_proj, v_proj, o_proj):
        import jax, jax.numpy as jnp
        import numpy as np
        B, T, C, D = (2, 2048, 512, 128)
        E = 8
        MIN_E = 2
        EPS = 1e-12
        NEG = -1000000000.0

        def _xavier(key, shape, fan_in, fan_out):
            bound = (6.0 / (fan_in + fan_out)) ** 0.5
            return jax.random.uniform(key, shape, jnp.float32, -bound, bound)

        def _forward(hidden_states, sim_matrix, gates, q_proj, k_proj, v_proj, o_proj):
            b, t, c = hidden_states.shape
            x = hidden_states.reshape(b * t, c)
            xn = x / jnp.maximum(jnp.linalg.norm(x, axis=-1, keepdims=True), EPS)
            sn = sim_matrix / jnp.maximum(jnp.linalg.norm(sim_matrix, axis=0, keepdims=True), EPS)
            logits = xn @ sn - jax.nn.sigmoid(gates)
            gated = jax.nn.relu(logits)
            mask = (gated > 0).astype(logits.dtype)
            inactive = jnp.sum(mask, axis=1) == 0
            top_idx = jax.lax.top_k(logits, MIN_E)[1]
            n = mask.shape[0]
            fb = jnp.zeros_like(mask).at[jnp.arange(n)[:, None], top_idx].set(1.0)
            mask = jnp.where(inactive[:, None] & (fb > 0), 1.0, mask)
            masked_logits = jnp.where(mask > 0, gated, NEG)
            routing_weights = jax.nn.softmax(masked_logits, axis=-1)
            m = jax.lax.stop_gradient(mask)
            q = jnp.einsum('tc,ecd,te->td', x, q_proj, m)
            k = jnp.einsum('tc,ecd,te->td', x, k_proj, m)
            v = jnp.einsum('tc,ecd,te->td', x, v_proj, m)
            qh = q.reshape(b, t, D)
            kh = k.reshape(b, t, D)
            vh = v.reshape(b, t, D)
            scores = jnp.einsum('bqd,bkd->bqk', qh, kh) / jnp.sqrt(jnp.asarray(D, qh.dtype))
            causal = jnp.tril(jnp.ones((t, t), bool))
            scores = jnp.where(causal, scores, jnp.finfo(scores.dtype).min)
            attn = jax.nn.softmax(scores, axis=-1)
            attn_out = jnp.einsum('bqk,bkd->bqd', attn, vh).reshape(b * t, D)
            final = jnp.einsum('td,edc,te->tc', attn_out, o_proj, m * routing_weights)
            return final.reshape(b, t, c)
        return _forward(hidden_states, sim_matrix, gates, q_proj, k_proj, v_proj, o_proj)
    x = x + _L0_ffn_ref(_L0_cond_ref(x, L0_cond_W1, L0_cond_b1, L0_cond_v, itok_B_0_2), L0_ffn_sim_matrix, L0_ffn_gates, L0_ffn_q_proj, L0_ffn_k_proj, L0_ffn_v_proj, L0_ffn_o_proj)
    return x

_drawn_inputs = setup_inputs


def setup_inputs(seed=0):
    import zlib

    import numpy as np

    out = dict(_drawn_inputs(seed))
    spreads = {'L0_ffn_gates': (0.0, 0.1)}
    factors = {'L0_cond_b1': 64.0, 'L0_ffn_q_proj': 3.636, 'L0_ffn_k_proj': 3.983}
    for name, (base, spread) in spreads.items():
        noise = np.random.default_rng([zlib.crc32(name.encode()), seed]).standard_normal(out[name].shape)
        drawn = base * np.exp(spread * noise) if base else spread * noise
        out[name] = jnp.asarray(drawn.astype(out[name].dtype))
    for name, factor in factors.items():
        out[name] = (out[name] * factor).astype(out[name].dtype)
    return out
```

```python
import concourse.bass as bass
from concourse import mybir
from contextlib import ExitStack


class Tile:

    RING = 6

    def __init__(self, lap, c):
        self.lap, self.c = lap, c

    def back(self, d):
        return Tile(self.lap, self.c - d)

    @property
    def n(self):
        return self.lap * self.RING + self.c

    def slot(self, ring):
        return self.c % ring

    def turn(self, ring):
        return self.lap * (self.RING // ring) + self.c // ring


def routed_ffn_kernel(nc: bass.Bass, x, itok, W1, b1, v, sim, gates, wq, wk, wv, wo, out):
    fp32, fp16, i32 = mybir.dt.float32, mybir.dt.float16, mybir.dt.int32
    ALU = mybir.AluOpType
    ACT = mybir.ActivationFunctionType
    AX = mybir.AxisListType

    B, S, C = x.shape
    P = 128
    A = W1.shape[1]
    E = sim.shape[1]
    D = wq.shape[2]
    NC = C // P
    D3 = 3 * D
    assert S == P and A == P and D == P
    EPS = 1e-12
    NEG = -1e30
    OFF = 1e9

    SX = 16.0
    SW = 64.0
    SA = 64.0
    ISQ = float(D) ** -0.5

    LAG_M, LAG_Q, LAG_A, LAG_O = 1, 2, 3, 4
    FIRST_FULL = LAG_O
    LAPS = (B - FIRST_FULL) // Tile.RING
    assert FIRST_FULL + LAPS * Tile.RING == B
    XR = Tile.RING

    ctx = ExitStack()
    with ctx:
        def sb(name, shape, dt=fp32):
            return ctx.enter_context(nc.sbuf_tensor(name, shape, dt))

        def pb(name, shape, dt=fp32):
            return ctx.enter_context(nc.psum_tensor(name, shape, dt))

        def sem(name):
            return ctx.enter_context(nc.semaphore(name))

        ident = sb("ident", [P, P])
        ident16 = sb("ident16", [P, P], fp16)
        ones = sb("ones", [P, P])
        after_j = sb("after_j", [P, S])
        before_j = sb("before_j", [P, S])
        at_j = sb("at_j", [P, S])
        tie = sb("tie", [P, E, E])
        half = sb("half", [P, 1])
        j_int = sb("j_int", [P, 1], i32)
        counts = sb("counts", [P, 3])
        itok_sb = sb("itok_sb", [P, B], i32)
        NT = 5
        kinds = sb("kinds", [P, B, NT])
        kinds_tmp = sb("kinds_tmp", [P, B])
        W1_raw = sb("W1_raw", [P, NC, A])
        W1_hi = sb("W1_hi", [P, NC, A], fp16)
        W1_lo = sb("W1_lo", [P, NC, A], fp16)
        b1_sb = sb("b1_sb", [P, 1])
        v_sb = sb("v_sb", [P, 1])
        v_wide = sb("v_wide", [P, P])
        sim_sb = sb("sim_sb", [P, NC, E])
        sim_sq = sb("sim_sq", [P, NC, E])
        sim_norm = sb("sim_norm", [P, E])
        sim_hi = sb("sim_hi", [P, NC, E], fp16)
        sim_lo = sb("sim_lo", [P, NC, E], fp16)
        halves = sb("halves", [P, E])
        sig = sb("sig", [P, E])
        WR = 2
        w_raw = sb("w_raw", [P, WR, NC * D3])
        wo_raw = sb("wo_raw", [P, WR, C])
        w_hi = sb("w_hi", [P, E, NC, D3], fp16)
        w_lo = sb("w_lo", [P, E, NC, D3], fp16)
        wo_hi = sb("wo_hi", [P, E, C], fp16)
        wo_lo = sb("wo_lo", [P, E, C], fp16)

        x_sb = sb("x_sb", [P, XR, C])
        KR = 3
        kind = sb("kind", [P, KR, NT])
        bias = sb("bias", [P, 2, S])
        bias_tmp = sb("bias_tmp", [P, S])
        xT_hi = sb("xT_hi", [P, NC, S], fp16)
        xT_lo = sb("xT_lo", [P, NC, S], fp16)
        h_sb = sb("h_sb", [P, S])
        s1 = sb("s1", [P, S])
        m1 = sb("m1", [P, 1])
        p1 = sb("p1", [P, S])
        sum1 = sb("sum1", [P, 2])
        p1T = sb("p1T", [P, S])
        pool_hl = sb("pool_hl", [P, 2, 2, NC * S], fp16)
        pool_sq = sb("pool_sq", [P, NC, S])
        lg = sb("lg", [P, E + 1])
        norm = sb("norm", [P, 4])
        logit = sb("logit", [P, E])
        diff = sb("diff", [P, E, E])
        beats = sb("beats", [P, E, E])
        rank = sb("rank", [P, E])
        top2 = sb("top2", [P, E])
        positive = sb("positive", [P, E])
        best = sb("best", [P, 3])
        gated = sb("gated", [P, E])
        masked = sb("masked", [P, E])
        rexp = sb("rexp", [P, E])
        rsum = sb("rsum", [P, 2])
        rw = sb("rw", [P, E])
        RR = 3
        route = sb("route", [P, RR, 3, E], fp16)
        mask_wide = sb("mask_wide", [P, E, S], fp16)
        pooled_e = sb("pooled_e", [P, 2, E, 2, NC * S], fp16)
        qkv = sb("qkv", [P, D3])
        qkT = sb("qkT", [P, 2, S])
        s2 = sb("s2", [P, S])
        m2 = sb("m2", [P, 1])
        p2 = sb("p2", [P, S])
        sum2 = sb("sum2", [P, 2])
        p2T = sb("p2T", [P, S])
        aoT = sb("aoT", [P, S])
        ao_e = sb("ao_e", [P, E, S])
        ao_hi = sb("ao_hi", [P, 2, E, S], fp16)
        ao_lo = sb("ao_lo", [P, 2, E, S], fp16)
        y_sb = sb("y_sb", [P, 2, C])

        ps_xT = pb("ps_xT", [P, NC, S])
        ps_pool = pb("ps_pool", [P, NC, S])
        ps_front = pb("ps_front", [P, 512])
        ps_attn = pb("ps_attn", [P, 512])
        ps_qkv = pb("ps_qkv", [P, 512])
        ps_out = pb("ps_out", [P, C])
        ps_wide = pb("ps_wide", [P, 2, 512])

        small_in = sem("small_in")
        w_in = [sem(f"w_in{i}") for i in range(WR)]
        consts_ready = sem("consts_ready")
        pool_setup = sem("pool_setup")
        dve_setup = sem("dve_setup")
        sim_sq_ready = sem("sim_sq_ready")
        sim_ss_ready = sem("sim_ss_ready")
        sim_ss_copied = sem("sim_ss_copied")
        sim_norm_ready = sem("sim_norm_ready")
        gate_exp_ready = sem("gate_exp_ready")
        kinds_ready = sem("kinds_ready")
        W1_hi_ready = sem("W1_hi_ready")
        setup_done = sem("setup_done")
        w_hi_ready = sem("w_hi_ready")
        w_split = sem("w_split")
        x_in = [sem(f"x_in{i}") for i in range(XR)]
        y_stored = [sem(f"y_stored{i}") for i in range(2)]
        pool_steps = sem("pool_steps")
        bias_ready = sem("bias_ready")
        norm_ready = sem("norm_ready")
        xT_ready = sem("xT_ready")
        xT_hi_ready = sem("xT_hi_ready")
        xT_split = sem("xT_split")
        h_ready = sem("h_ready")
        tanh_done = sem("tanh_done")
        score_ready = sem("score_ready")
        front_steps = sem("front_steps")
        max1_ready = sem("max1_ready")
        exp1_done = sem("exp1_done")
        p1_ready = sem("p1_ready")
        p1T_ready = sem("p1T_ready")
        p1T_copied = sem("p1T_copied")
        pool_ready = sem("pool_ready")
        pool_hi_ready = sem("pool_hi_ready")
        pool_sq_ready = sem("pool_sq_ready")
        pool_split = sem("pool_split")
        lg_ready = sem("lg_ready")
        lg_copied = sem("lg_copied")
        route_steps = sem("route_steps")
        masked_ready = sem("masked_ready")
        rexp_done = sem("rexp_done")
        route_ready = sem("route_ready")
        mask_ready = sem("mask_ready")
        mask_copied = sem("mask_copied")
        pooled_e_ready = sem("pooled_e_ready")
        qkv_ready = sem("qkv_ready")
        qkv_copied = sem("qkv_copied")
        qkT_ready = sem("qkT_ready")
        qkT_copied = sem("qkT_copied")
        s2_ready = sem("s2_ready")
        attn_steps = sem("attn_steps")
        max2_ready = sem("max2_ready")
        exp2_done = sem("exp2_done")
        p2_ready = sem("p2_ready")
        p2T_ready = sem("p2T_ready")
        p2T_copied = sem("p2T_copied")
        weight_wide_ready = sem("weight_wide_ready")
        ao_ready = sem("ao_ready")
        ao_copied = sem("ao_copied")
        ao_e_ready = sem("ao_e_ready")
        ao_hi_ready = sem("ao_hi_ready")
        ao_split = sem("ao_split")
        out_ready = sem("out_ready")
        y_ready = sem("y_ready")

        SMALL_DMAS = 6

        def after(eng, semaphore, value):
            if not isinstance(value, int) or value > 0:
                eng.wait_ge(semaphore, value)

        def slots(eng, one_slot):
            def at(lap, c, peeled):
                stages = [Tile(lap, c - lag) for lag in (0, LAG_M, LAG_Q, LAG_A, LAG_O)]
                if peeled:
                    stages = [t if 0 <= t.n < B else None for t in stages]
                one_slot(*stages)
            for c in range(FIRST_FULL):
                at(0, c, True)
            with eng.Fori(0, LAPS) as lap:
                for u in range(Tile.RING):
                    at(lap, FIRST_FULL + u, False)
            for c in range(FIRST_FULL, FIRST_FULL + LAG_O):
                at(LAPS, c, True)

        block = ctx.enter_context(nc.Block())

        @block.sync
        def _(sp):
            sp.dma_start(W1_raw[:], W1.rearrange("(c p) a -> p c a", p=P)).then_inc(small_in, 16)
            sp.dma_start(x_sb[:, 0, :], x[0, :, :]).then_inc(x_in[0], 16)
            sp.dma_start(sim_sb[:], sim.rearrange("(c p) e -> p c e", p=P)).then_inc(small_in, 16)
            sp.dma_start(b1_sb[:], b1.rearrange("(a o) -> a o", o=1)).then_inc(small_in, 16)
            sp.dma_start(v_sb[:], v.rearrange("(a o) -> a o", o=1)).then_inc(small_in, 16)
            sp.dma_start(itok_sb[:], itok.rearrange("(o b) -> o b", o=1).broadcast_to([P, B])).then_inc(small_in, 16)
            sp.dma_start(sig[:], gates.rearrange("(o e) -> o e", o=1).broadcast_to([P, E])).then_inc(small_in, 16)
            sp.dma_start(x_sb[:, 1, :], x[1, :, :]).then_inc(x_in[1], 16)

            for e in range(E):
                after(sp, w_split, e - WR + 1)
                raw = w_raw[:, e % WR, :].rearrange("p (c t d) -> p c t d", c=NC, t=3)
                for t, w in enumerate((wq, wk, wv)):
                    sp.dma_start(raw[:, :, t, :], w[e, :, :].rearrange("(c p) d -> p c d", p=P))\
                      .then_inc(w_in[e % WR], 16)
                sp.dma_start(wo_raw[:, e % WR, :], wo[e, :, :]).then_inc(w_in[e % WR], 16)

            def slot(F, M, Q, A_, O):
                if O is not None:
                    sp.wait_ge(y_ready, O.n + 2)
                    sp.dma_start(out[bass.ds(O.n, 1), :, :].rearrange("o s c -> (o s) c"),
                                 y_sb[:, O.slot(2), :]).then_inc(y_stored[O.slot(2)], 16)
                if F is None:
                    return
                ahead = F.back(-2)
                if isinstance(ahead.n, int) and ahead.n >= B:
                    return
                sp.dma_start(x_sb[:, ahead.slot(XR), :],
                             x[bass.ds(ahead.n, 1), :, :].rearrange("o s c -> (o s) c"))\
                  .then_inc(x_in[ahead.slot(XR)], 16)

            def at(lap, c, peeled):
                stages = [Tile(lap, c - lag) for lag in (0, LAG_M, LAG_Q, LAG_A, LAG_O)]
                if peeled:
                    stages = [t if 0 <= t.n < B else None for t in stages]
                slot(*stages)
            for c in range(FIRST_FULL):
                at(0, c, True)
            with sp.Fori(0, LAPS - 1) as lap:
                for u in range(Tile.RING):
                    at(lap, FIRST_FULL + u, False)
            for c in range(FIRST_FULL, FIRST_FULL + Tile.RING + LAG_O):
                at(LAPS - 1, c, True)
            for par in range(2):
                sp.wait_ge(y_stored[par], 16 * (B // 2 + 1))

        @block.gpsimd
        def _(pool):
            steps = [0]

            def link(ins):
                steps[0] += 1
                ins.then_inc(pool_setup, 1)
                pool.wait_ge(pool_setup, steps[0])

            link(pool.memset(ident[:], 0.0))
            link(pool.affine_select(out=ident[:], in_=ident[:], compare_op=ALU.not_equal, fill=1.0, base=0,
                                    pattern=[[-1, P]], channel_multiplier=1))
            link(pool.tensor_copy(ident16[:], ident[:]))
            link(pool.memset(ones[:], 1.0))
            link(pool.memset(after_j[:], 0.0))
            link(pool.memset(before_j[:], 0.0))
            link(pool.memset(at_j[:], 0.0))
            link(pool.affine_select(out=after_j[:], in_=after_j[:], compare_op=ALU.is_ge, fill=NEG, base=0,
                                    pattern=[[-1, S]], channel_multiplier=1))
            link(pool.affine_select(out=before_j[:], in_=before_j[:], compare_op=ALU.is_ge, fill=NEG, base=0,
                                    pattern=[[1, S]], channel_multiplier=-1))
            link(pool.affine_select(out=at_j[:], in_=at_j[:], compare_op=ALU.not_equal, fill=NEG, base=0,
                                    pattern=[[-1, S]], channel_multiplier=1))
            link(pool.memset(tie[:], 0.0))
            link(pool.affine_select(out=tie[:], in_=tie[:], compare_op=ALU.is_ge, fill=-1e-37, base=0,
                                    pattern=[[-1, E], [1, E]], channel_multiplier=0))
            link(pool.memset(half[:], 0.5))
            link(pool.memset(halves[:], 0.5))
            pool.iota(j_int[:], pattern=[[0, 1]], base=0, channel_multiplier=1).then_inc(consts_ready, 1)
            pool.wait_ge(sim_ss_copied, 1)
            pool.tensor_tensor(out=sim_norm[:], in0=sim_norm[:], in1=halves[:], op=ALU.pow).then_inc(sim_norm_ready, 1)
            pool.wait_ge(kinds_ready, 1)

            BIAS_STEPS = 5

            def slot(F, M, Q, A_, O):
                if F is None:
                    return
                kcol = kind[:, F.slot(KR), :]
                count = [0]

                def link(ins):
                    count[0] += 1
                    ins.then_inc(pool_steps, 1)
                    pool.wait_ge(pool_steps, F.n * BIAS_STEPS + count[0])

                after(pool, qkv_copied, F.n + 1 - KR)
                link(pool.tensor_copy(kcol, kinds[:, bass.ds(F.n, 1), :].rearrange("p o t -> p (o t)")))
                after(pool, max1_ready, F.n - 1)
                b = bias[:, F.slot(2), :]
                link(pool.tensor_tensor(out=b, in0=after_j[:], in1=kcol[:, 0:1].broadcast_to([P, S]), op=ALU.mult))
                link(pool.tensor_tensor(out=bias_tmp[:], in0=before_j[:], in1=kcol[:, 1:2].broadcast_to([P, S]), op=ALU.mult))
                link(pool.tensor_tensor(out=b, in0=b, in1=bias_tmp[:], op=ALU.add))
                link(pool.tensor_tensor(out=bias_tmp[:], in0=at_j[:], in1=kcol[:, 2:3].broadcast_to([P, S]), op=ALU.mult))
                pool.tensor_tensor(out=b, in0=b, in1=bias_tmp[:], op=ALU.add).then_inc(bias_ready, 1)
                assert count[0] == BIAS_STEPS
                pool.wait_ge(lg_copied, F.n + 1)
                pool.tensor_tensor(out=norm[:, 0:1], in0=lg[:, E:E + 1], in1=half[:], op=ALU.pow)\
                    .then_inc(norm_ready, 1)

            slots(pool, slot)

        @block.scalar
        def _(act):
            act.wait_ge(small_in, 16 * SMALL_DMAS)
            act.activation(W1_hi[:], W1_raw[:], ACT.Copy, scale=SW).then_inc(W1_hi_ready, 1)
            act.activation(sig[:], sig[:], ACT.Exp, scale=-1.0).then_inc(gate_exp_ready, 1)
            for e in range(E):
                act.wait_ge(w_in[e % WR], 64 * (e // WR + 1))
                act.activation(w_hi[:, e, :, :].rearrange("p c n -> p (c n)"), w_raw[:, e % WR, :], ACT.Copy,
                               scale=SW)
                act.activation(wo_hi[:, e, :], wo_raw[:, e % WR, :], ACT.Copy, scale=SW).then_inc(w_hi_ready, 1)
            act.wait_ge(setup_done, 1)

            def slot(F, M, Q, A_, O):
                if F is not None:
                    act.wait_ge(xT_ready, F.n + 1)
                    act.activation(xT_hi[:], ps_xT[:], ACT.Copy, scale=SX).then_inc(xT_hi_ready, 1)
                if M is not None:
                    act.wait_ge(mask_ready, M.n + 1)
                    after(act, pooled_e_ready, M.n * E)
                    act.activation(mask_wide[:].rearrange("p e s -> p (e s)"),
                                   ps_wide[:].rearrange("p h n -> p (h n)"), ACT.Copy).then_inc(mask_copied, 1)
                if F is not None:
                    act.wait_ge(h_ready, F.n + 1)
                    act.activation(h_sb[:], ps_front[:, 0:S], ACT.Tanh, bias=b1_sb[:], scale=1.0 / (SX * SW))\
                        .then_inc(tanh_done, 1)
                if A_ is not None:
                    act.wait_ge(qkT_ready, A_.n + 1)
                    act.activation(qkT[:].rearrange("p t s -> p (t s)"), ps_attn[:, 0:2 * S], ACT.Copy)\
                        .then_inc(qkT_copied, 1)
                if F is not None:
                    act.wait_ge(max1_ready, F.n + 1)
                    act.activation(p1[:], s1[:], ACT.Exp, bias=m1[:], accum_out=sum1[:, 0:1])\
                        .then_inc(exp1_done, 1)
                if A_ is not None:
                    act.wait_ge(max2_ready, A_.n + 1)
                    act.activation(p2[:], s2[:], ACT.Exp, bias=m2[:], accum_out=sum2[:, 0:1])\
                        .then_inc(exp2_done, 1)
                if F is not None:
                    act.wait_ge(p1T_ready, F.n + 1)
                    act.activation(p1T[:], ps_front[:, 0:S], ACT.Copy).then_inc(p1T_copied, 1)
                if A_ is not None:
                    act.wait_ge(p2T_ready, A_.n + 1)
                    act.activation(p2T[:], ps_attn[:, 0:S], ACT.Copy).then_inc(p2T_copied, 1)
                if F is not None:
                    act.wait_ge(pool_ready, F.n + 1)
                    after(act, pooled_e_ready, (F.n - 1) * E)
                    act.activation(pool_hl[:, F.slot(2), 0, :], ps_pool[:].rearrange("p c s -> p (c s)"), ACT.Copy,
                                   scale=SX).then_inc(pool_hi_ready, 1)
                    act.activation(pool_sq[:], ps_pool[:], ACT.Square).then_inc(pool_sq_ready, 1)
                if A_ is not None:
                    act.wait_ge(ao_ready, A_.n + 1)
                    act.activation(aoT[:], ps_attn[:, 0:S], ACT.Copy).then_inc(ao_copied, 1)
                    act.wait_ge(ao_e_ready, A_.n + 1)
                    act.activation(ao_hi[:, A_.slot(2), :, :], ao_e[:], ACT.Copy).then_inc(ao_hi_ready, 1)
                if F is not None:
                    act.wait_ge(masked_ready, F.n + 1)
                    act.activation(rexp[:], masked[:], ACT.Exp, bias=best[:, 2:3], accum_out=rsum[:, 0:1])\
                        .then_inc(rexp_done, 1)
                if Q is not None:
                    act.wait_ge(qkv_ready, Q.n + 1)
                    act.activation(qkv[:], ps_qkv[:, 0:D3], ACT.Identity, scale=kind[:, Q.slot(KR), 4:5])\
                        .then_inc(qkv_copied, 1)

            slots(act, slot)

        @block.vector
        def _(dve):
            steps = [0]

            def link(ins):
                steps[0] += 1
                ins.then_inc(dve_setup, 1)
                dve.wait_ge(dve_setup, steps[0])

            dve.wait_ge(small_in, 16 * SMALL_DMAS)
            dve.tensor_tensor(out=sim_sq[:], in0=sim_sb[:], in1=sim_sb[:], op=ALU.mult).then_inc(sim_sq_ready, 1)
            dve.wait_ge(W1_hi_ready, 1)
            dve.scalar_tensor_tensor(out=W1_lo[:], in0=W1_raw[:], scalar=SW, in1=W1_hi[:], op0=ALU.mult,
                                     op1=ALU.subtract)
            dve.wait_ge(consts_ready, 1)
            dve.tensor_scalar(v_wide[:], ones[:], v_sb[:], None, ALU.mult)
            link(dve.tensor_copy(counts[:, 0:1], j_int[:]))
            link(dve.tensor_scalar(counts[:, 1:2], counts[:, 0:1], -1.0, float(S), ALU.mult, ALU.add))
            link(dve.tensor_scalar(counts[:, 0:1], counts[:, 0:1], 1.0, None, ALU.add))
            link(dve.memset(counts[:, 2:3], float(S - 1)))
            link(dve.reciprocal(counts[:], counts[:]))
            link(dve.tensor_copy(kinds_tmp[:], itok_sb[:]))
            link(dve.tensor_scalar(kinds[:, :, 0], kinds_tmp[:], 0.0, None, ALU.is_equal))
            link(dve.tensor_scalar(kinds[:, :, 1], kinds_tmp[:], 1.0, None, ALU.is_equal))
            link(dve.tensor_tensor(out=kinds[:, :, 2], in0=kinds[:, :, 0], in1=kinds[:, :, 1], op=ALU.add))
            link(dve.tensor_scalar(kinds[:, :, 2], kinds[:, :, 2], -1.0, 1.0, ALU.mult, ALU.add))
            link(dve.tensor_scalar(kinds[:, :, 3], kinds[:, :, 0], counts[:, 0:1], None, ALU.mult))
            link(dve.scalar_tensor_tensor(out=kinds_tmp[:], in0=kinds[:, :, 1], scalar=counts[:, 1:2],
                                          in1=kinds[:, :, 3], op0=ALU.mult, op1=ALU.add))
            link(dve.scalar_tensor_tensor(out=kinds[:, :, 3], in0=kinds[:, :, 2], scalar=counts[:, 2:3],
                                          in1=kinds_tmp[:], op0=ALU.mult, op1=ALU.add))
            dve.tensor_scalar(kinds[:, :, 4], kinds[:, :, 3], 1.0 / (SX * SW), None, ALU.mult)\
               .then_inc(kinds_ready, 1)
            dve.wait_ge(sim_ss_ready, 1)
            dve.tensor_copy(sim_norm[:], ps_front[:, 0:E]).then_inc(sim_ss_copied, 1)
            dve.wait_ge(sim_norm_ready, 1)
            link(dve.tensor_scalar(sim_norm[:], sim_norm[:], EPS, None, ALU.max))
            link(dve.reciprocal(sim_norm[:], sim_norm[:]))
            for c in range(NC):
                last = dve.tensor_tensor(out=sim_sb[:, c, :], in0=sim_sb[:, c, :], in1=sim_norm[:], op=ALU.mult)
            link(last)
            link(dve.tensor_scalar(sim_sb[:], sim_sb[:], SW, None, ALU.mult))
            link(dve.tensor_copy(sim_hi[:], sim_sb[:]))
            link(dve.tensor_tensor(out=sim_lo[:], in0=sim_sb[:], in1=sim_hi[:], op=ALU.subtract))
            dve.wait_ge(gate_exp_ready, 1)
            link(dve.tensor_scalar(sig[:], sig[:], 1.0, None, ALU.add))
            dve.reciprocal(sig[:], sig[:]).then_inc(setup_done, 1)
            dve.wait_ge(setup_done, 1)
            for par in range(2):
                dve.sem_inc(y_stored[par], 16)
            dve.sem_inc(y_ready, 1)
            for e in range(E):
                dve.wait_ge(w_hi_ready, e + 1)
                dve.scalar_tensor_tensor(out=w_lo[:, e, :, :].rearrange("p c n -> p (c n)"),
                                         in0=w_raw[:, e % WR, :], scalar=SW,
                                         in1=w_hi[:, e, :, :].rearrange("p c n -> p (c n)"),
                                         op0=ALU.mult, op1=ALU.subtract)
                dve.scalar_tensor_tensor(out=wo_lo[:, e, :], in0=wo_raw[:, e % WR, :], scalar=SW,
                                         in1=wo_hi[:, e, :], op0=ALU.mult, op1=ALU.subtract).then_inc(w_split, 1)

            FRONT_STEPS, ATTN_STEPS, ROUTE_STEPS = 2, 2, 16

            def linker(semaphore, tile, per_tile):
                count = [0]

                def link(ins):
                    count[0] += 1
                    assert count[0] <= per_tile
                    ins.then_inc(semaphore, 1)
                    dve.wait_ge(semaphore, tile.n * per_tile + count[0])
                return link

            def slot(F, M, Q, A_, O):
                front = F and linker(front_steps, F, FRONT_STEPS)
                attn = A_ and linker(attn_steps, A_, ATTN_STEPS)

                def mask_experts(first, end):
                    if M is None:
                        return
                    for e in range(first, end):
                        if e == 0:
                            dve.wait_ge(mask_copied, M.n + 1)
                            dve.wait_ge(pool_split, M.n + 1)
                            after(dve, qkv_ready, M.n - 1)
                        dve.tensor_tensor(
                            out=pooled_e[:, M.slot(2), e, :, :].rearrange("p h (c s) -> p (h c) s", s=S),
                            in0=pool_hl[:, M.slot(2), :, :].rearrange("p h (c s) -> p (h c) s", s=S),
                            in1=mask_wide[:, e:e + 1, :].broadcast_to([P, 2 * NC, S]),
                            op=ALU.mult).then_inc(pooled_e_ready, 1)

                if F is not None:
                    dve.wait_ge(xT_hi_ready, F.n + 1)
                    dve.scalar_tensor_tensor(out=xT_lo[:], in0=ps_xT[:], scalar=SX, in1=xT_hi[:],
                                             op0=ALU.mult, op1=ALU.subtract).then_inc(xT_split, 1)
                mask_experts(0, 2)
                if F is not None:
                    dve.wait_ge(score_ready, F.n + 1)
                    dve.wait_ge(bias_ready, F.n + 1)
                    front(dve.tensor_tensor(out=s1[:], in0=ps_front[:, 0:S], in1=bias[:, F.slot(2), :], op=ALU.add))
                    dve.tensor_reduce(out=m1[:], in_=s1[:], axis=AX.X, op=ALU.max, negate=True)\
                       .then_inc(max1_ready, 1)
                if A_ is not None:
                    dve.wait_ge(s2_ready, A_.n + 1)
                    attn(dve.scalar_tensor_tensor(out=s2[:], in0=ps_attn[:, 0:S], scalar=ISQ, in1=after_j[:],
                                                  op0=ALU.mult, op1=ALU.add))
                    dve.tensor_reduce(out=m2[:], in_=s2[:], axis=AX.X, op=ALU.max, negate=True)\
                       .then_inc(max2_ready, 1)
                mask_experts(2, 4)
                if F is not None:
                    dve.wait_ge(exp1_done, F.n + 1)
                    front(dve.reciprocal(sum1[:, 1:2], sum1[:, 0:1]))
                    dve.tensor_scalar(p1[:], p1[:], sum1[:, 1:2], None, ALU.mult).then_inc(p1_ready, 1)
                if A_ is not None:
                    dve.wait_ge(exp2_done, A_.n + 1)
                    attn(dve.reciprocal(sum2[:, 1:2], sum2[:, 0:1]))
                    dve.tensor_scalar(p2[:], p2[:], sum2[:, 1:2], None, ALU.mult).then_inc(p2_ready, 1)
                mask_experts(4, 6)
                if F is not None:
                    dve.wait_ge(pool_sq_ready, F.n + 1)
                    dve.scalar_tensor_tensor(out=pool_hl[:, F.slot(2), 1, :],
                                             in0=ps_pool[:].rearrange("p c s -> p (c s)"), scalar=SX,
                                             in1=pool_hl[:, F.slot(2), 0, :], op0=ALU.mult, op1=ALU.subtract)\
                       .then_inc(pool_split, 1)
                if A_ is not None:
                    dve.wait_ge(weight_wide_ready, A_.n + 1)
                    dve.wait_ge(ao_copied, A_.n + 1)
                    dve.tensor_tensor(out=ao_e[:], in0=ps_wide[:].rearrange("p h (e s) -> p (h e) s", s=S),
                                      in1=aoT[:].rearrange("p (o s) -> p o s", o=1).broadcast_to([P, E, S]),
                                      op=ALU.mult).then_inc(ao_e_ready, 1)
                mask_experts(6, 8)
                if A_ is not None:
                    dve.wait_ge(ao_hi_ready, A_.n + 1)
                    dve.tensor_tensor(out=ao_lo[:, A_.slot(2), :, :], in0=ao_e[:], in1=ao_hi[:, A_.slot(2), :, :],
                                      op=ALU.subtract).then_inc(ao_split, 1)
                if O is not None:
                    dve.wait_ge(out_ready, O.n + 1)
                    dve.wait_ge(y_stored[O.slot(2)], 16 * O.turn(2) + 16)
                    dve.scalar_tensor_tensor(out=y_sb[:, O.slot(2), :], in0=ps_out[:], scalar=1.0 / (SA * SW),
                                             in1=x_sb[:, O.slot(XR), :], op0=ALU.mult, op1=ALU.add)\
                       .then_inc(y_ready, 1)
                if F is not None:
                    router(F)

            def router(F):
                link = linker(route_steps, F, ROUTE_STEPS)
                icount = kind[:, F.slot(KR), 3:4]
                icount_unscaled = kind[:, F.slot(KR), 4:5]
                r = F.slot(RR)
                dve.wait_ge(lg_ready, F.n + 1)
                dve.tensor_copy(lg[:], ps_front[:, 0:E + 1]).then_inc(lg_copied, 1)
                dve.wait_ge(norm_ready, F.n + 1)
                link(dve.tensor_scalar(norm[:, 1:2], norm[:, 0:1], icount, EPS, ALU.mult, ALU.max))
                link(dve.reciprocal(norm[:, 2:3], norm[:, 1:2]))
                link(dve.tensor_scalar(norm[:, 3:4], norm[:, 2:3], icount_unscaled, None, ALU.mult))
                link(dve.scalar_tensor_tensor(out=logit[:], in0=lg[:, 0:E], scalar=norm[:, 3:4], in1=sig[:],
                                              op0=ALU.mult, op1=ALU.subtract))
                link(dve.tensor_tensor(out=diff[:],
                                       in0=logit[:].rearrange("p (o e) -> p o e", o=1).broadcast_to([P, E, E]),
                                       in1=logit[:].rearrange("p (e o) -> p e o", o=1).broadcast_to([P, E, E]),
                                       op=ALU.subtract))
                link(dve.tensor_tensor(out=beats[:], in0=diff[:], in1=tie[:], op=ALU.is_gt))
                link(dve.tensor_reduce(out=rank[:], in_=beats[:], axis=AX.X, op=ALU.add))
                link(dve.tensor_reduce(out=best[:, 0:1], in_=logit[:], axis=AX.X, op=ALU.max))
                link(dve.tensor_scalar(best[:, 1:2], best[:, 0:1], 0.0, None, ALU.is_le))
                link(dve.tensor_scalar(top2[:], rank[:], 2.0, best[:, 1:2], ALU.is_lt, ALU.mult))
                link(dve.tensor_scalar(positive[:], logit[:], 0.0, None, ALU.is_gt))
                link(dve.tensor_tensor(out=route[:, r, 0, :], in0=top2[:], in1=positive[:], op=ALU.max))
                link(dve.scalar_tensor_tensor(out=gated[:], in0=logit[:], scalar=0.0, in1=route[:, r, 0, :],
                                              op0=ALU.max, op1=ALU.mult))
                dve.tensor_scalar(best[:, 2:3], best[:, 0:1], -1.0, 0.0, ALU.mult, ALU.min)
                link(dve.tensor_scalar(masked[:], route[:, r, 0, :], -1.0, OFF, ALU.add, ALU.mult))
                dve.tensor_tensor(out=masked[:], in0=masked[:], in1=gated[:], op=ALU.add)\
                   .then_inc(masked_ready, 1)
                dve.wait_ge(rexp_done, F.n + 1)
                link(dve.reciprocal(rsum[:, 1:2], rsum[:, 0:1]))
                dve.tensor_scalar(rw[:], rexp[:], rsum[:, 1:2], SA, ALU.mult, ALU.mult)
                link(dve.tensor_scalar(route[:, r, 1, :], rexp[:], rsum[:, 1:2], SA, ALU.mult, ALU.mult))
                dve.tensor_tensor(out=route[:, r, 2, :], in0=rw[:], in1=route[:, r, 1, :], op=ALU.subtract)\
                   .then_inc(route_ready, 1)

            slots(dve, slot)

        @block.tensor
        def _(pe):
            pe.wait_ge(consts_ready, 1)
            pe.wait_ge(sim_sq_ready, 1)
            for c in range(NC):
                last = pe.matmul(ps_front[:, 0:E], ones[:], sim_sq[:, c, :], start=(c == 0), stop=(c == NC - 1))
            last.then_inc(sim_ss_ready, 1)
            pe.wait_ge(setup_done, 1)

            def transpose_x(F):
                pe.wait_ge(x_in[F.slot(XR)], 16 * F.turn(XR) + 16)
                for c in range(NC):
                    last = pe.transpose(ps_xT[:, c, :], x_sb[:, F.slot(XR), c * P:(c + 1) * P], ident[:])
                last.then_inc(xT_ready, 1)

            def split_products(psum, pairs, semaphore):
                for i, (left, right) in enumerate(pairs):
                    last = pe.matmul(psum, left, right, start=(i == 0), stop=(i == len(pairs) - 1))
                last.then_inc(semaphore, 1)

            def hidden(F):
                pe.wait_ge(xT_split, F.n + 1)
                split_products(ps_front[:, 0:S],
                               [(w[:, c, :], t[:, c, :]) for c in range(NC)
                                for w, t in ((W1_hi, xT_hi), (W1_hi, xT_lo), (W1_lo, xT_hi))], h_ready)

            def scores(F):
                pe.wait_ge(tanh_done, F.n + 1)
                pe.matmul(ps_front[:, 0:S], v_wide[:], h_sb[:], start=True, stop=True).then_inc(score_ready, 1)

            def transpose_p1(F):
                pe.wait_ge(p1_ready, F.n + 1)
                pe.transpose(ps_front[:, 0:S], p1[:], ident[:]).then_inc(p1T_ready, 1)

            def pooling(F):
                pe.wait_ge(p1T_copied, F.n + 1)
                for c in range(NC):
                    last = pe.matmul(ps_pool[:, c, :], x_sb[:, F.slot(XR), c * P:(c + 1) * P], p1T[:],
                                     start=True, stop=True)
                last.then_inc(pool_ready, 1)

            def router_products(F):
                pe.wait_ge(pool_split, F.n + 1)
                hi = pool_hl[:, F.slot(2), 0, :].rearrange("p (c s) -> p c s", c=NC)
                lo = pool_hl[:, F.slot(2), 1, :].rearrange("p (c s) -> p c s", c=NC)
                pairs = [(a[:, c, :], b[:, c, :]) for c in range(NC)
                         for a, b in ((hi, sim_hi), (hi, sim_lo), (lo, sim_hi))]
                for i, (a, b) in enumerate(pairs):
                    pe.matmul(ps_front[:, 0:E], a, b, start=(i == 0), stop=(i == len(pairs) - 1))
                for c in range(NC):
                    last = pe.matmul(ps_front[:, E:E + 1], pool_sq[:, c, :], ones[:, 0:1],
                                     start=(c == 0), stop=(c == NC - 1))
                last.then_inc(lg_ready, 1)

            def widen_mask(M):
                pe.wait_ge(route_ready, M.n + 1)
                after(pe, ao_e_ready, M.n - (LAG_A - LAG_M))
                for e in range(E):
                    last = pe.matmul(ps_wide[:, e // 4, (e % 4) * S:(e % 4 + 1) * S],
                                     route[:, M.slot(RR), 0, e:e + 1].broadcast_to([P, P]), ident16[:],
                                     start=True, stop=True)
                last.then_inc(mask_ready, 1)

            def widen_weights(A_, M):
                if M is not None:
                    pe.wait_ge(mask_copied, M.n + 1)
                for e in range(E):
                    for h in (1, 2):
                        last = pe.matmul(ps_wide[:, e // 4, (e % 4) * S:(e % 4 + 1) * S],
                                         route[:, A_.slot(RR), h, e:e + 1].broadcast_to([P, P]), ident16[:],
                                         start=(h == 1), stop=(h == 2))
                last.then_inc(weight_wide_ready, 1)

            def qkv_expert(Q, e):
                pe.wait_ge(pooled_e_ready, Q.n * E + e + 1)
                if e == 0:
                    after(pe, qkv_copied, Q.n)
                if isinstance(Q.n, int) and Q.n == 0:
                    pe.wait_ge(w_split, e + 1)
                for c in range(NC):
                    hi = pooled_e[:, Q.slot(2), e, 0, c * S:(c + 1) * S]
                    lo = pooled_e[:, Q.slot(2), e, 1, c * S:(c + 1) * S]
                    for i, (a, b) in enumerate(((hi, w_hi), (hi, w_lo), (lo, w_hi))):
                        last = pe.matmul(ps_qkv[:, 0:D3], a, b[:, e, c, :], start=(e == 0 and c == 0 and i == 0),
                                         stop=(e == E - 1 and c == NC - 1 and i == 2))
                if e == E - 1:
                    last.then_inc(qkv_ready, 1)

            def transpose_qk(A_):
                pe.wait_ge(qkv_copied, A_.n + 1)
                pe.transpose(ps_attn[:, 0:S], qkv[:, 0:D], ident[:])
                pe.transpose(ps_attn[:, S:2 * S], qkv[:, D:2 * D], ident[:]).then_inc(qkT_ready, 1)

            def attention_scores(A_):
                pe.wait_ge(qkT_copied, A_.n + 1)
                pe.matmul(ps_attn[:, 0:S], qkT[:, 0, :], qkT[:, 1, :], start=True, stop=True).then_inc(s2_ready, 1)

            def transpose_p2(A_):
                pe.wait_ge(p2_ready, A_.n + 1)
                pe.transpose(ps_attn[:, 0:S], p2[:], ident[:]).then_inc(p2T_ready, 1)

            def attention_output(A_):
                pe.wait_ge(p2T_copied, A_.n + 1)
                pe.matmul(ps_attn[:, 0:S], qkv[:, 2 * D:D3], p2T[:], start=True, stop=True).then_inc(ao_ready, 1)

            def out_expert(O, e):
                if e == 0:
                    pe.wait_ge(ao_split, O.n + 1)
                    pe.wait_ge(y_ready, O.n + 1)
                hi, lo = ao_hi[:, O.slot(2), e, :], ao_lo[:, O.slot(2), e, :]
                for i, (a, b) in enumerate(((hi, wo_hi), (hi, wo_lo), (lo, wo_hi))):
                    last = pe.matmul(ps_out[:], a, b[:, e, :], start=(e == 0 and i == 0), stop=(e == E - 1 and i == 2))
                if e == E - 1:
                    last.then_inc(out_ready, 1)

            def slot(F, M, Q, A_, O):
                def q(*experts):
                    for e in experts if Q is not None else ():
                        qkv_expert(Q, e)

                def o(*experts):
                    for e in experts if O is not None else ():
                        out_expert(O, e)

                def run(step, tile, *more):
                    if tile is not None:
                        step(tile, *more)

                run(transpose_x, F)
                q(0)
                run(widen_mask, M)
                run(hidden, F)
                run(transpose_qk, A_)
                q(1)
                o(0, 1)
                run(scores, F)
                run(attention_scores, A_)
                q(2)
                o(2, 3)
                q(3)
                run(transpose_p1, F)
                run(transpose_p2, A_)
                run(widen_weights, A_, M)
                q(4)
                o(4)
                run(pooling, F)
                run(attention_output, A_)
                q(5)
                o(5, 6, 7)
                run(router_products, F)
                q(6, 7)

            slots(pe, slot)


_INS = ['x', 'itok_B_0_2', 'L0_cond_W1', 'L0_cond_b1', 'L0_cond_v', 'L0_ffn_sim_matrix', 'L0_ffn_gates',
        'L0_ffn_q_proj', 'L0_ffn_k_proj', 'L0_ffn_v_proj', 'L0_ffn_o_proj']


def kernel(**inputs):
    import numpy as _np
    import concourse.bacc as _bacc
    from concourse import mybir as _mybir
    from concourse.bass_utils import run_bass_kernel_spmd as _run

    nc = _bacc.Bacc("TRN2", target_bir_lowering=False, num_devices=1)
    arrays, args = {}, []
    for name in _INS:
        a = _np.ascontiguousarray(inputs[name])
        arrays[f"in_{name}_dram"] = a
        args.append(nc.dram_tensor(f"in_{name}_dram", a.shape, _mybir.dt.from_np(a.dtype), kind="ExternalInput").ap())
    shape = inputs['x'].shape
    args.append(nc.dram_tensor("out_0_dram", shape, _mybir.dt.float32, kind="ExternalOutput").ap())
    routed_ffn_kernel(nc, *args)
    r = _run(nc, [arrays], core_ids=[0])
    return r.results[0]["out_0_dram"]
```

```python
import concourse.bass as bass
from concourse import mybir
from contextlib import ExitStack


class Tile:

    RING = 6

    def __init__(self, lap, c):
        self.lap, self.c = lap, c

    def back(self, d):
        return Tile(self.lap, self.c - d)

    @property
    def n(self):
        return self.lap * self.RING + self.c

    def slot(self, ring):
        return self.c % ring

    def turn(self, ring):
        return self.lap * (self.RING // ring) + self.c // ring


def routed_ffn_kernel(nc: bass.Bass, x, itok, W1, b1, v, sim, gates, wq, wk, wv, wo, out):
    fp32, fp16, i32 = mybir.dt.float32, mybir.dt.float16, mybir.dt.int32
    bf16 = mybir.dt.bfloat16
    ALU = mybir.AluOpType
    ACT = mybir.ActivationFunctionType
    AX = mybir.AxisListType

    B, S, C = x.shape
    P = 128
    A = W1.shape[1]
    E = sim.shape[1]
    D = wq.shape[2]
    NC = C // P
    D3 = 3 * D
    assert S == P and A == P and D == P
    EPS = 1e-12
    NEG = -1e30
    OFF = 1e9

    SX = 16.0
    SW = 64.0
    SA = 64.0
    ISQ = float(D) ** -0.5

    LAGS = (0, 1, 2, 3, 4, 5)
    LAG_M, LAG_A, LAG_O = LAGS[2], LAGS[4], LAGS[5]
    LOOP_FROM = LAG_O + (B - LAG_O) % Tile.RING
    LAPS = (B - LOOP_FROM) // Tile.RING
    XR = Tile.RING

    ctx = ExitStack()
    with ctx:
        def sb(name, shape, dt=fp32):
            return ctx.enter_context(nc.sbuf_tensor(name, shape, dt))

        def pb(name, shape, dt=fp32):
            return ctx.enter_context(nc.psum_tensor(name, shape, dt))

        def sem(name):
            return ctx.enter_context(nc.semaphore(name))

        ident = sb("ident", [P, P])
        ident16 = sb("ident16", [P, P], fp16)
        ones = sb("ones", [P, P])
        after_j = sb("after_j", [P, S])
        before_j = sb("before_j", [P, S])
        at_j = sb("at_j", [P, S])
        tie = sb("tie", [P, E, E])
        half = sb("half", [P, 1])
        j_int = sb("j_int", [P, 1], i32)
        counts = sb("counts", [P, 3])
        itok_sb = sb("itok_sb", [P, B], i32)
        NT = 5
        kinds = sb("kinds", [P, B, NT])
        kinds_tmp = sb("kinds_tmp", [P, B])
        W1_raw = sb("W1_raw", [P, NC, A])
        W1_hi = sb("W1_hi", [P, NC, A], fp16)
        W1_lo = sb("W1_lo", [P, NC, A], fp16)
        b1_sb = sb("b1_sb", [P, 1])
        v_sb = sb("v_sb", [P, 1])
        v_wide = sb("v_wide", [P, P])
        sim_sb = sb("sim_sb", [P, NC, E])
        sim_sq = sb("sim_sq", [P, NC, E])
        sim_norm = sb("sim_norm", [P, E])
        sim_hi = sb("sim_hi", [P, NC, E], fp16)
        sim_lo = sb("sim_lo", [P, NC, E], fp16)
        halves = sb("halves", [P, E])
        bit_e = sb("bit_e", [P, E])
        ones16 = sb("ones16", [P, P], fp16)
        ones_bf = sb("ones_bf", [P, 1], bf16)
        zeros16 = sb("zeros16", [P, C], fp16)
        sig = sb("sig", [P, E])
        WR = 3
        w_raw = sb("w_raw", [P, WR, NC * D3])
        wo_raw = sb("wo_raw", [P, WR, C])
        w_hi = sb("w_hi", [P, E, NC, D3], fp16)
        w_lo = sb("w_lo", [P, E, NC, D3], fp16)
        wo_hi = sb("wo_hi", [P, E, C], fp16)
        wo_lo = sb("wo_lo", [P, E, C], fp16)

        x_sb = sb("x_sb", [P, XR, C])
        kind = sb("kind", [P, XR, NT])
        bias = sb("bias", [P, 2, S])
        bias_tmp = sb("bias_tmp", [P, S])
        xT_hi = sb("xT_hi", [P, NC, S], fp16)
        xT_lo = sb("xT_lo", [P, NC, S], fp16)
        h_sb = sb("h_sb", [P, S])
        s1 = sb("s1", [P, S])
        m1 = sb("m1", [P, 1])
        p1 = sb("p1", [P, S])
        sum1 = sb("sum1", [P, 2])
        p1T = sb("p1T", [P, S])
        PR = 3
        pool_hl = sb("pool_hl", [P, PR, 2, NC * S], fp16)
        pool_sq = sb("pool_sq", [P, NC, S])
        sq_hi = sb("sq_hi", [P, NC, S], bf16)
        sq_lo = sb("sq_lo", [P, NC, S], bf16)
        lg = sb("lg", [P, E + 1])
        norm = sb("norm", [P, 4])
        logit = sb("logit", [P, E])
        diff = sb("diff", [P, E, E])
        beats = sb("beats", [P, E, E])
        rank = sb("rank", [P, E])
        top2 = sb("top2", [P, E])
        positive = sb("positive", [P, E])
        best = sb("best", [P, 3])
        gated = sb("gated", [P, E])
        masked = sb("masked", [P, E])
        rexp = sb("rexp", [P, E])
        rsum = sb("rsum", [P, 2])
        rw = sb("rw", [P, E])
        route = sb("route", [P, XR, 3, E], fp16)
        active = sb("active", [P, E])
        active_bits = sb("active_bits", [P, XR], i32)
        mask_wide = sb("mask_wide", [P, E, S], fp16)
        pooled_e = sb("pooled_e", [P, 2, E, 2, NC * S], fp16)
        qkv = sb("qkv", [P, D3])
        qkT = sb("qkT", [P, 2, S])
        s2 = sb("s2", [P, S])
        m2 = sb("m2", [P, 1])
        p2 = sb("p2", [P, S])
        sum2 = sb("sum2", [P, 2])
        p2T = sb("p2T", [P, S])
        aoT = sb("aoT", [P, S])
        ao_e = sb("ao_e", [P, E, S])
        ao_hi = sb("ao_hi", [P, 2, E, S], fp16)
        ao_lo = sb("ao_lo", [P, 2, E, S], fp16)
        y_sb = sb("y_sb", [P, 2, C])

        ps_tall = pb("ps_tall", [P, NC, S])
        ps_front = pb("ps_front", [P, 512])
        ps_attn = pb("ps_attn", [P, 512])
        ps_qkv = [pb(f"ps_qkv{i}", [P, 512]) for i in range(2)]
        ps_out = pb("ps_out", [P, C])
        ps_wide = pb("ps_wide", [P, 2, 512])

        small_in = sem("small_in")
        w_in = [sem(f"w_in{i}") for i in range(WR)]
        consts_ready = sem("consts_ready")
        pool_setup = sem("pool_setup")
        dve_setup = sem("dve_setup")
        sim_sq_ready = sem("sim_sq_ready")
        sim_ss_ready = sem("sim_ss_ready")
        sim_ss_copied = sem("sim_ss_copied")
        sim_norm_ready = sem("sim_norm_ready")
        gate_exp_ready = sem("gate_exp_ready")
        kinds_ready = sem("kinds_ready")
        W1_hi_ready = sem("W1_hi_ready")
        setup_done = sem("setup_done")
        w_hi_ready = sem("w_hi_ready")
        w_split = sem("w_split")
        x_in = [sem(f"x_in{i}") for i in range(XR)]
        y_stored = [sem(f"y_stored{i}") for i in range(2)]
        pool_steps = sem("pool_steps")
        bias_ready = sem("bias_ready")
        norm_ready = sem("norm_ready")
        xT_ready = sem("xT_ready")
        xT_hi_ready = sem("xT_hi_ready")
        xT_split = sem("xT_split")
        h_ready = sem("h_ready")
        tanh_done = sem("tanh_done")
        score_ready = sem("score_ready")
        front_steps = sem("front_steps")
        max1_ready = sem("max1_ready")
        exp1_done = sem("exp1_done")
        p1_ready = sem("p1_ready")
        p1T_ready = sem("p1T_ready")
        p1T_copied = sem("p1T_copied")
        pool_ready = sem("pool_ready")
        pool_hi_ready = sem("pool_hi_ready")
        pool_sq_ready = sem("pool_sq_ready")
        sq_hi_ready = sem("sq_hi_ready")
        sq_split = sem("sq_split")
        pool_split = sem("pool_split")
        lg_ready = sem("lg_ready")
        lg_copied = sem("lg_copied")
        route_steps = sem("route_steps")
        bit_steps = sem("bit_steps")
        masked_ready = sem("masked_ready")
        rexp_done = sem("rexp_done")
        route_ready = sem("route_ready")
        mask_ready = sem("mask_ready")
        mask_copied = sem("mask_copied")
        pooled_e_ready = sem("pooled_e_ready")
        counts_ready = sem("counts_ready")
        bits_ready = sem("bits_ready")
        bits_seen = sem("bits_seen")
        qkv_ready = sem("qkv_ready")
        qkv_copied = sem("qkv_copied")
        qkT_ready = sem("qkT_ready")
        qkT_copied = sem("qkT_copied")
        s2_ready = sem("s2_ready")
        attn_steps = sem("attn_steps")
        max2_ready = sem("max2_ready")
        exp2_done = sem("exp2_done")
        p2_ready = sem("p2_ready")
        p2T_ready = sem("p2T_ready")
        p2T_copied = sem("p2T_copied")
        weight_wide_ready = sem("weight_wide_ready")
        ao_ready = sem("ao_ready")
        ao_copied = sem("ao_copied")
        ao_e_ready = sem("ao_e_ready")
        ao_hi_ready = sem("ao_hi_ready")
        ao_split = sem("ao_split")
        out_ready = sem("out_ready")
        y_ready = sem("y_ready")

        SMALL_DMAS = 6

        def after(eng, semaphore, value):
            if not isinstance(value, int) or value > 0:
                eng.wait_ge(semaphore, value)

        def stages(lap, c, peeled):
            tiles = [Tile(lap, c - lag) for lag in LAGS]
            return [None if peeled and not 0 <= t.n < B else t for t in tiles]

        def slots(eng, one_slot, laps=LAPS):
            for c in range(LOOP_FROM):
                one_slot(*stages(0, c, True))
            with eng.Fori(0, laps) as lap:
                for u in range(Tile.RING):
                    one_slot(*stages(lap, LOOP_FROM + u, False))
            for c in range(LOOP_FROM, B + LAG_O - laps * Tile.RING):
                one_slot(*stages(laps, c, True))

        block = ctx.enter_context(nc.Block())

        @block.sync
        def _(sp):
            sp.dma_start(W1_raw[:], W1.rearrange("(c p) a -> p c a", p=P)).then_inc(small_in, 16)
            sp.dma_start(x_sb[:, 0, :], x[0, :, :]).then_inc(x_in[0], 16)
            sp.dma_start(sim_sb[:], sim.rearrange("(c p) e -> p c e", p=P)).then_inc(small_in, 16)
            sp.dma_start(b1_sb[:], b1.rearrange("(a o) -> a o", o=1)).then_inc(small_in, 16)
            sp.dma_start(v_sb[:], v.rearrange("(a o) -> a o", o=1)).then_inc(small_in, 16)
            sp.dma_start(itok_sb[:], itok.rearrange("(o b) -> o b", o=1).broadcast_to([P, B])).then_inc(small_in, 16)
            sp.dma_start(sig[:], gates.rearrange("(o e) -> o e", o=1).broadcast_to([P, E])).then_inc(small_in, 16)

            sp.dma_start(x_sb[:, 1, :], x[1, :, :]).then_inc(x_in[1], 16)
            for e in range(E):
                after(sp, w_split, e - WR + 1)
                raw = w_raw[:, e % WR, :].rearrange("p (c t d) -> p c t d", c=NC, t=3)
                for t, w in enumerate((wq, wk, wv)):
                    sp.dma_start(raw[:, :, t, :], w[e, :, :].rearrange("(c p) d -> p c d", p=P))\
                      .then_inc(w_in[e % WR], 16)
                sp.dma_start(wo_raw[:, e % WR, :], wo[e, :, :]).then_inc(w_in[e % WR], 16)
                if 2 <= e < XR:
                    sp.dma_start(x_sb[:, e, :], x[e, :, :]).then_inc(x_in[e], 16)

            def slot(F, R, M, Q, A_, O):
                if O is not None:
                    sp.wait_ge(y_ready, O.n + 1)
                    sp.dma_start(out[bass.ds(O.n, 1), :, :].rearrange("o s c -> (o s) c"),
                                 y_sb[:, O.slot(2), :]).then_inc(y_stored[O.slot(2)], 16)
                if F is None or (isinstance(F.n, int) and F.n + 1 == B):
                    return
                ahead = F.back(-1)
                if isinstance(ahead.n, int) and ahead.n < XR:
                    return
                sp.dma_start(x_sb[:, ahead.slot(XR), :],
                             x[bass.ds(ahead.n, 1), :, :].rearrange("o s c -> (o s) c"))\
                  .then_inc(x_in[ahead.slot(XR)], 16)

            slots(sp, slot, LAPS - 1)
            for par in range(2):
                sp.wait_ge(y_stored[par], 16 * (B // 2))

        @block.gpsimd
        def _(pool):
            steps = [0]

            def link(ins):
                steps[0] += 1
                ins.then_inc(pool_setup, 1)
                pool.wait_ge(pool_setup, steps[0])

            link(pool.memset(ident[:], 0.0))
            link(pool.affine_select(out=ident[:], in_=ident[:], compare_op=ALU.not_equal, fill=1.0, base=0,
                                    pattern=[[-1, P]], channel_multiplier=1))
            link(pool.tensor_copy(ident16[:], ident[:]))
            link(pool.memset(ones[:], 1.0))
            link(pool.memset(after_j[:], 0.0))
            link(pool.memset(before_j[:], 0.0))
            link(pool.memset(at_j[:], 0.0))
            link(pool.affine_select(out=after_j[:], in_=after_j[:], compare_op=ALU.is_ge, fill=NEG, base=0,
                                    pattern=[[-1, S]], channel_multiplier=1))
            link(pool.affine_select(out=before_j[:], in_=before_j[:], compare_op=ALU.is_ge, fill=NEG, base=0,
                                    pattern=[[1, S]], channel_multiplier=-1))
            link(pool.affine_select(out=at_j[:], in_=at_j[:], compare_op=ALU.not_equal, fill=NEG, base=0,
                                    pattern=[[-1, S]], channel_multiplier=1))
            link(pool.memset(tie[:], 0.0))
            link(pool.affine_select(out=tie[:], in_=tie[:], compare_op=ALU.is_ge, fill=-1e-37, base=0,
                                    pattern=[[-1, E], [1, E]], channel_multiplier=0))
            link(pool.memset(half[:], 0.5))
            link(pool.memset(halves[:], 0.5))
            for e in range(E):
                last = pool.memset(bit_e[:, e:e + 1], float(2 ** e))
            link(last)
            link(pool.memset(ones16[:], 1.0))
            link(pool.memset(zeros16[:], 0.0))
            link(pool.memset(ones_bf[:], 1.0))
            pool.iota(j_int[:], pattern=[[0, 1]], base=0, channel_multiplier=1).then_inc(consts_ready, 1)
            pool.wait_ge(sim_ss_copied, 1)
            pool.tensor_tensor(out=sim_norm[:], in0=sim_norm[:], in1=halves[:], op=ALU.pow).then_inc(sim_norm_ready, 1)
            pool.wait_ge(kinds_ready, 1)

            BIAS_STEPS = 5

            def slot(F, R, M, Q, A_, O):
                if R is not None:
                    pool.wait_ge(lg_copied, R.n + 1)
                    pool.tensor_tensor(out=norm[:, 0:1], in0=lg[:, E:E + 1], in1=half[:], op=ALU.pow)\
                        .then_inc(norm_ready, 1)
                if F is None:
                    return
                kcol = kind[:, F.slot(XR), :]
                count = [0]

                def link(ins):
                    count[0] += 1
                    ins.then_inc(pool_steps, 1)
                    pool.wait_ge(pool_steps, F.n * BIAS_STEPS + count[0])

                after(pool, qkv_copied, F.n + 1 - XR)
                link(pool.tensor_copy(kcol, kinds[:, bass.ds(F.n, 1), :].rearrange("p o t -> p (o t)")))
                after(pool, max1_ready, F.n - 1)
                b = bias[:, F.slot(2), :]
                link(pool.tensor_tensor(out=b, in0=after_j[:], in1=kcol[:, 0:1].broadcast_to([P, S]), op=ALU.mult))
                link(pool.tensor_tensor(out=bias_tmp[:], in0=before_j[:], in1=kcol[:, 1:2].broadcast_to([P, S]), op=ALU.mult))
                link(pool.tensor_tensor(out=b, in0=b, in1=bias_tmp[:], op=ALU.add))
                link(pool.tensor_tensor(out=bias_tmp[:], in0=at_j[:], in1=kcol[:, 2:3].broadcast_to([P, S]), op=ALU.mult))
                pool.tensor_tensor(out=b, in0=b, in1=bias_tmp[:], op=ALU.add).then_inc(bias_ready, 1)
                assert count[0] == BIAS_STEPS
                pool.wait_ge(sq_hi_ready, F.n + 1)
                pool.tensor_tensor(out=sq_lo[:], in0=pool_sq[:], in1=sq_hi[:], op=ALU.subtract).then_inc(sq_split, 1)

            slots(pool, slot)

        @block.scalar
        def _(act):
            act.wait_ge(small_in, 16 * SMALL_DMAS)
            act.activation(W1_hi[:], W1_raw[:], ACT.Copy, scale=SW).then_inc(W1_hi_ready, 1)
            act.activation(sig[:], sig[:], ACT.Exp, scale=-1.0).then_inc(gate_exp_ready, 1)

            def weight_high(e):
                act.wait_ge(w_in[e % WR], 64 * (e // WR + 1))
                act.activation(w_hi[:, e, :, :].rearrange("p c n -> p (c n)"), w_raw[:, e % WR, :], ACT.Copy,
                               scale=SW)
                act.activation(wo_hi[:, e, :], wo_raw[:, e % WR, :], ACT.Copy, scale=SW).then_inc(w_hi_ready, 1)
            act.wait_ge(setup_done, 1)

            def weight_part(Q, F, part):
                if Q is None and F is not None and F.n * 3 + part < E:
                    weight_high(F.n * 3 + part)

            def slot(F, R, M, Q, A_, O):
                if F is not None:
                    act.wait_ge(xT_ready, F.n + 1)
                    act.activation(xT_hi[:], ps_tall[:], ACT.Copy, scale=SX).then_inc(xT_hi_ready, 1)
                if M is not None:
                    act.wait_ge(mask_ready, M.n + 1)
                    after(act, pooled_e_ready, M.n * E)
                    act.activation(mask_wide[:].rearrange("p e s -> p (e s)"),
                                   ps_wide[:].rearrange("p h n -> p (h n)"), ACT.Copy).then_inc(mask_copied, 1)
                weight_part(Q, F, 0)
                if F is not None:
                    act.wait_ge(h_ready, F.n + 1)
                    act.activation(h_sb[:], ps_front[:, 0:S], ACT.Tanh, bias=b1_sb[:], scale=1.0 / (SX * SW))\
                        .then_inc(tanh_done, 1)
                if A_ is not None:
                    act.wait_ge(qkT_ready, A_.n + 1)
                    act.activation(qkT[:].rearrange("p t s -> p (t s)"), ps_attn[:, 0:2 * S], ACT.Copy)\
                        .then_inc(qkT_copied, 1)
                if F is not None:
                    act.wait_ge(max1_ready, F.n + 1)
                    act.activation(p1[:], s1[:], ACT.Exp, bias=m1[:], accum_out=sum1[:, 0:1])\
                        .then_inc(exp1_done, 1)
                if A_ is not None:
                    act.wait_ge(max2_ready, A_.n + 1)
                    act.activation(p2[:], s2[:], ACT.Exp, bias=m2[:], accum_out=sum2[:, 0:1])\
                        .then_inc(exp2_done, 1)
                weight_part(Q, F, 1)
                if F is not None:
                    act.wait_ge(p1T_ready, F.n + 1)
                    act.activation(p1T[:], ps_front[:, 0:S], ACT.Copy).then_inc(p1T_copied, 1)
                if A_ is not None:
                    act.wait_ge(p2T_ready, A_.n + 1)
                    act.activation(p2T[:], ps_attn[:, 0:S], ACT.Copy).then_inc(p2T_copied, 1)
                if R is not None:
                    act.wait_ge(masked_ready, R.n + 1)
                    act.activation(rexp[:], masked[:], ACT.Exp, bias=best[:, 2:3], accum_out=rsum[:, 0:1])\
                        .then_inc(rexp_done, 1)
                weight_part(Q, F, 2)
                if F is not None:
                    act.wait_ge(pool_ready, F.n + 1)
                    after(act, pooled_e_ready, (F.n + 1 - PR) * E)
                    act.activation(pool_hl[:, F.slot(PR), 0, :], ps_tall[:].rearrange("p c s -> p (c s)"), ACT.Copy,
                                   scale=SX).then_inc(pool_hi_ready, 1)
                    after(act, sq_split, F.n)
                    act.activation(pool_sq[:], ps_tall[:], ACT.Square).then_inc(pool_sq_ready, 1)
                    after(act, lg_ready, F.n)
                    act.wait_ge(pool_sq_ready, F.n + 1)
                    act.activation(sq_hi[:], pool_sq[:], ACT.Copy).then_inc(sq_hi_ready, 1)
                if A_ is not None:
                    act.wait_ge(ao_ready, A_.n + 1)
                    act.activation(aoT[:], ps_attn[:, 0:S], ACT.Copy).then_inc(ao_copied, 1)
                    act.wait_ge(ao_e_ready, A_.n + 1)
                    act.activation(ao_hi[:, A_.slot(2), :, :], ao_e[:], ACT.Copy).then_inc(ao_hi_ready, 1)
                if Q is not None:
                    act.wait_ge(qkv_ready, Q.n + 1)
                    act.activation(qkv[:], ps_qkv[Q.slot(2)][:, 0:D3], ACT.Identity, scale=kind[:, Q.slot(XR), 4:5])\
                        .then_inc(qkv_copied, 1)

            slots(act, slot)

        @block.vector
        def _(dve):
            steps = [0]

            def link(ins):
                steps[0] += 1
                ins.then_inc(dve_setup, 1)
                dve.wait_ge(dve_setup, steps[0])

            dve.wait_ge(small_in, 16 * SMALL_DMAS)
            dve.tensor_tensor(out=sim_sq[:], in0=sim_sb[:], in1=sim_sb[:], op=ALU.mult).then_inc(sim_sq_ready, 1)
            dve.wait_ge(W1_hi_ready, 1)
            dve.scalar_tensor_tensor(out=W1_lo[:], in0=W1_raw[:], scalar=SW, in1=W1_hi[:], op0=ALU.mult,
                                     op1=ALU.subtract)
            dve.wait_ge(consts_ready, 1)
            dve.tensor_scalar(v_wide[:], ones[:], v_sb[:], None, ALU.mult)
            link(dve.tensor_copy(counts[:, 0:1], j_int[:]))
            link(dve.tensor_scalar(counts[:, 1:2], counts[:, 0:1], -1.0, float(S), ALU.mult, ALU.add))
            link(dve.tensor_scalar(counts[:, 0:1], counts[:, 0:1], 1.0, None, ALU.add))
            link(dve.memset(counts[:, 2:3], float(S - 1)))
            link(dve.reciprocal(counts[:], counts[:]))
            link(dve.tensor_copy(kinds_tmp[:], itok_sb[:]))
            link(dve.tensor_scalar(kinds[:, :, 0], kinds_tmp[:], 0.0, None, ALU.is_equal))
            link(dve.tensor_scalar(kinds[:, :, 1], kinds_tmp[:], 1.0, None, ALU.is_equal))
            link(dve.tensor_tensor(out=kinds[:, :, 2], in0=kinds[:, :, 0], in1=kinds[:, :, 1], op=ALU.add))
            link(dve.tensor_scalar(kinds[:, :, 2], kinds[:, :, 2], -1.0, 1.0, ALU.mult, ALU.add))
            link(dve.tensor_scalar(kinds[:, :, 3], kinds[:, :, 0], counts[:, 0:1], None, ALU.mult))
            link(dve.scalar_tensor_tensor(out=kinds_tmp[:], in0=kinds[:, :, 1], scalar=counts[:, 1:2],
                                          in1=kinds[:, :, 3], op0=ALU.mult, op1=ALU.add))
            link(dve.scalar_tensor_tensor(out=kinds[:, :, 3], in0=kinds[:, :, 2], scalar=counts[:, 2:3],
                                          in1=kinds_tmp[:], op0=ALU.mult, op1=ALU.add))
            dve.tensor_scalar(kinds[:, :, 4], kinds[:, :, 3], 1.0 / (SX * SW), None, ALU.mult)\
               .then_inc(kinds_ready, 1)
            dve.wait_ge(sim_ss_ready, 1)
            dve.tensor_copy(sim_norm[:], ps_front[:, 0:E]).then_inc(sim_ss_copied, 1)
            dve.wait_ge(sim_norm_ready, 1)
            link(dve.tensor_scalar(sim_norm[:], sim_norm[:], EPS, None, ALU.max))
            link(dve.reciprocal(sim_norm[:], sim_norm[:]))
            for c in range(NC):
                last = dve.tensor_tensor(out=sim_sb[:, c, :], in0=sim_sb[:, c, :], in1=sim_norm[:], op=ALU.mult)
            link(last)
            link(dve.tensor_scalar(sim_sb[:], sim_sb[:], SW, None, ALU.mult))
            link(dve.tensor_copy(sim_hi[:], sim_sb[:]))
            link(dve.tensor_tensor(out=sim_lo[:], in0=sim_sb[:], in1=sim_hi[:], op=ALU.subtract))
            dve.wait_ge(gate_exp_ready, 1)
            link(dve.tensor_scalar(sig[:], sig[:], 1.0, None, ALU.add))
            dve.reciprocal(sig[:], sig[:]).then_inc(setup_done, 1)
            dve.wait_ge(setup_done, 1)

            def weight_low(e):
                dve.wait_ge(w_hi_ready, e + 1)
                dve.scalar_tensor_tensor(out=w_lo[:, e, :, :].rearrange("p c n -> p (c n)"),
                                         in0=w_raw[:, e % WR, :], scalar=SW,
                                         in1=w_hi[:, e, :, :].rearrange("p c n -> p (c n)"),
                                         op0=ALU.mult, op1=ALU.subtract)
                dve.scalar_tensor_tensor(out=wo_lo[:, e, :], in0=wo_raw[:, e % WR, :], scalar=SW,
                                         in1=wo_hi[:, e, :], op0=ALU.mult, op1=ALU.subtract).then_inc(w_split, 1)

            def weight_part(Q, F, part):
                if Q is None and F is not None and F.n * 3 + part < E:
                    weight_low(F.n * 3 + part)

            FRONT_STEPS, ATTN_STEPS, BIT_STEPS, ROUTE_STEPS = 2, 2, 1, 12

            class Steps:

                def __init__(self, semaphore, tile, per_tile):
                    self.semaphore, self.tile, self.per_tile, self.count = semaphore, tile, per_tile, 0

                def mark(self, ins):
                    self.count += 1
                    assert self.count <= self.per_tile
                    ins.then_inc(self.semaphore, 1)

                def wait(self):
                    dve.wait_ge(self.semaphore, self.tile.n * self.per_tile + self.count)

            def mask_experts(M, first, end):
                if M is None:
                    return
                for e in range(first, end):
                    if e == 0:
                        dve.wait_ge(mask_copied, M.n + 1)
                        after(dve, qkv_ready, M.n - 1)
                    dve.tensor_tensor(
                        out=pooled_e[:, M.slot(2), e, :, :].rearrange("p h (c s) -> p (h c) s", s=S),
                        in0=pool_hl[:, M.slot(PR), :, :].rearrange("p h (c s) -> p (h c) s", s=S),
                        in1=mask_wide[:, e:e + 1, :].broadcast_to([P, 2 * NC, S]),
                        op=ALU.mult).then_inc(pooled_e_ready, 1)

            def expert_bits(M):
                if M is None:
                    return
                steps = Steps(bit_steps, M, BIT_STEPS)
                dve.wait_ge(counts_ready, M.n + 1)
                steps.mark(dve.scalar_tensor_tensor(out=active[:], in0=ps_front[:, 0:E], scalar=0.5, in1=bit_e[:],
                                                    op0=ALU.is_gt, op1=ALU.mult))
                steps.wait()
                with nc.allow_low_precision("small integers"):
                    dve.tensor_reduce(out=active_bits[:, M.slot(XR):M.slot(XR) + 1], in_=active[:], axis=AX.X,
                                      op=ALU.add).then_inc(bits_ready, 1)

            def xT_low(F):
                dve.wait_ge(xT_hi_ready, F.n + 1)
                dve.scalar_tensor_tensor(out=xT_lo[:], in0=ps_tall[:], scalar=SX, in1=xT_hi[:],
                                         op0=ALU.mult, op1=ALU.subtract).then_inc(xT_split, 1)

            def masked_scores(F, A_):
                if F is not None:
                    front = Steps(front_steps, F, FRONT_STEPS)
                    dve.wait_ge(score_ready, F.n + 1)
                    dve.wait_ge(bias_ready, F.n + 1)
                    front.mark(dve.tensor_tensor(out=s1[:], in0=ps_front[:, 0:S], in1=bias[:, F.slot(2), :],
                                                 op=ALU.add))
                if A_ is not None:
                    attn = Steps(attn_steps, A_, ATTN_STEPS)
                    dve.wait_ge(s2_ready, A_.n + 1)
                    attn.mark(dve.scalar_tensor_tensor(out=s2[:], in0=ps_attn[:, 0:S], scalar=ISQ, in1=after_j[:],
                                                       op0=ALU.mult, op1=ALU.add))
                if F is not None:
                    front.wait()
                    dve.tensor_reduce(out=m1[:], in_=s1[:], axis=AX.X, op=ALU.max, negate=True)\
                       .then_inc(max1_ready, 1)
                if A_ is not None:
                    attn.wait()
                    dve.tensor_reduce(out=m2[:], in_=s2[:], axis=AX.X, op=ALU.max, negate=True)\
                       .then_inc(max2_ready, 1)

            def normalise(F, A_):
                if F is not None:
                    front = Steps(front_steps, F, FRONT_STEPS)
                    front.count = 1
                    dve.wait_ge(exp1_done, F.n + 1)
                    front.mark(dve.reciprocal(sum1[:, 1:2], sum1[:, 0:1]))
                if A_ is not None:
                    attn = Steps(attn_steps, A_, ATTN_STEPS)
                    attn.count = 1
                    dve.wait_ge(exp2_done, A_.n + 1)
                    attn.mark(dve.reciprocal(sum2[:, 1:2], sum2[:, 0:1]))
                if F is not None:
                    front.wait()
                    dve.tensor_scalar(p1[:], p1[:], sum1[:, 1:2], None, ALU.mult).then_inc(p1_ready, 1)
                if A_ is not None:
                    attn.wait()
                    dve.tensor_scalar(p2[:], p2[:], sum2[:, 1:2], None, ALU.mult).then_inc(p2_ready, 1)

            def pooled_low(F):
                dve.wait_ge(pool_sq_ready, F.n + 1)
                dve.scalar_tensor_tensor(out=pool_hl[:, F.slot(PR), 1, :],
                                         in0=ps_tall[:].rearrange("p c s -> p (c s)"), scalar=SX,
                                         in1=pool_hl[:, F.slot(PR), 0, :], op0=ALU.mult, op1=ALU.subtract)\
                   .then_inc(pool_split, 1)

            def weighted_attention(A_):
                dve.wait_ge(weight_wide_ready, A_.n + 1)
                dve.wait_ge(ao_copied, A_.n + 1)
                dve.tensor_tensor(out=ao_e[:], in0=ps_wide[:].rearrange("p h (e s) -> p (h e) s", s=S),
                                  in1=aoT[:].rearrange("p (o s) -> p o s", o=1).broadcast_to([P, E, S]),
                                  op=ALU.mult).then_inc(ao_e_ready, 1)

            def weighted_low(A_):
                dve.wait_ge(ao_hi_ready, A_.n + 1)
                dve.tensor_tensor(out=ao_lo[:, A_.slot(2), :, :], in0=ao_e[:], in1=ao_hi[:, A_.slot(2), :, :],
                                  op=ALU.subtract).then_inc(ao_split, 1)

            def add_x(O):
                dve.wait_ge(out_ready, O.n + 1)
                after(dve, y_stored[O.slot(2)], 16 * O.turn(2))
                dve.scalar_tensor_tensor(out=y_sb[:, O.slot(2), :], in0=ps_out[:], scalar=1.0 / (SA * SW),
                                         in1=x_sb[:, O.slot(XR), :], op0=ALU.mult, op1=ALU.add)\
                   .then_inc(y_ready, 1)

            class Router:

                def __init__(self, R):
                    self.R = R
                    self.steps = Steps(route_steps, R, ROUTE_STEPS)
                    self.mask, self.w_hi, self.w_lo = (route[:, R.slot(XR), i, :] for i in range(3))

                def take_products(self):
                    dve.wait_ge(lg_ready, self.R.n + 1)
                    dve.tensor_copy(lg[:], ps_front[:, 0:E + 1]).then_inc(lg_copied, 1)

                def guarded_norm(self):
                    dve.wait_ge(norm_ready, self.R.n + 1)
                    self.steps.mark(dve.tensor_scalar(norm[:, 1:2], norm[:, 0:1], kind[:, self.R.slot(XR), 3:4], EPS,
                                                      ALU.mult, ALU.max))

                def inverse_norm(self):
                    self.steps.wait()
                    self.steps.mark(dve.reciprocal(norm[:, 2:3], norm[:, 1:2]))

                def logit_scale(self):
                    self.steps.wait()
                    self.steps.mark(dve.tensor_scalar(norm[:, 3:4], norm[:, 2:3], kind[:, self.R.slot(XR), 4:5], None,
                                                      ALU.mult))

                def logits(self):
                    self.steps.wait()
                    self.steps.mark(dve.scalar_tensor_tensor(out=logit[:], in0=lg[:, 0:E], scalar=norm[:, 3:4],
                                                             in1=sig[:], op0=ALU.mult, op1=ALU.subtract))

                def differences(self):
                    self.steps.wait()
                    dve.tensor_tensor(out=diff[:],
                                      in0=logit[:].rearrange("p (o e) -> p o e", o=1).broadcast_to([P, E, E]),
                                      in1=logit[:].rearrange("p (e o) -> p e o", o=1).broadcast_to([P, E, E]),
                                      op=ALU.subtract)
                    dve.tensor_scalar(positive[:], logit[:], 0.0, None, ALU.is_gt)
                    self.steps.mark(dve.tensor_reduce(out=best[:, 0:1], in_=logit[:], axis=AX.X, op=ALU.max))

                def comparisons(self):
                    self.steps.wait()
                    dve.tensor_tensor(out=beats[:], in0=diff[:], in1=tie[:], op=ALU.is_gt)
                    dve.tensor_scalar(best[:, 2:3], best[:, 0:1], -1.0, 0.0, ALU.mult, ALU.min)
                    self.steps.mark(dve.tensor_scalar(best[:, 1:2], best[:, 0:1], 0.0, None, ALU.is_le))

                def ranks(self):
                    self.steps.wait()
                    self.steps.mark(dve.tensor_reduce(out=rank[:], in_=beats[:], axis=AX.X, op=ALU.add))

                def two_best(self):
                    self.steps.wait()
                    self.steps.mark(dve.tensor_scalar(top2[:], rank[:], 2.0, best[:, 1:2], ALU.is_lt, ALU.mult))

                def set_mask(self):
                    self.steps.wait()
                    self.steps.mark(dve.tensor_tensor(out=self.mask, in0=top2[:], in1=positive[:], op=ALU.max))

                def gate(self):
                    self.steps.wait()
                    dve.scalar_tensor_tensor(out=gated[:], in0=logit[:], scalar=0.0, in1=self.mask,
                                             op0=ALU.max, op1=ALU.mult)
                    self.steps.mark(dve.tensor_scalar(masked[:], self.mask, -1.0, OFF, ALU.add, ALU.mult))

                def masked_logits(self):
                    self.steps.wait()
                    dve.tensor_tensor(out=masked[:], in0=masked[:], in1=gated[:], op=ALU.add)\
                       .then_inc(masked_ready, 1)

                def inverse_sum(self):
                    dve.wait_ge(rexp_done, self.R.n + 1)
                    self.steps.mark(dve.reciprocal(rsum[:, 1:2], rsum[:, 0:1]))

                def weights(self):
                    self.steps.wait()
                    dve.tensor_scalar(rw[:], rexp[:], rsum[:, 1:2], SA, ALU.mult, ALU.mult)
                    self.steps.mark(dve.tensor_scalar(self.w_hi, rexp[:], rsum[:, 1:2], SA, ALU.mult, ALU.mult))

                def weights_low(self):
                    self.steps.wait()
                    dve.tensor_tensor(out=self.w_lo, in0=rw[:], in1=self.w_hi, op=ALU.subtract)\
                       .then_inc(route_ready, 1)
                    assert self.steps.count == ROUTE_STEPS

            def slot(F, R, M, Q, A_, O):
                def run(step, tile):
                    if tile is not None:
                        step(tile)

                router = Router(R) if R is not None else None

                def route_step(step):
                    if router is not None:
                        step(router)

                run(xT_low, F)
                route_step(Router.take_products)
                weight_part(Q, F, 0)
                run(expert_bits, M)
                mask_experts(M, 0, 1)
                route_step(Router.guarded_norm)
                mask_experts(M, 1, 2)
                route_step(Router.inverse_norm)
                route_step(Router.logit_scale)
                route_step(Router.logits)
                masked_scores(F, A_)
                route_step(Router.differences)
                mask_experts(M, 2, 3)
                normalise(F, A_)
                route_step(Router.comparisons)
                weight_part(Q, F, 1)
                route_step(Router.ranks)
                mask_experts(M, 3, 4)
                route_step(Router.two_best)
                route_step(Router.set_mask)
                route_step(Router.gate)
                route_step(Router.masked_logits)
                mask_experts(M, 4, 6)
                run(add_x, O)
                route_step(Router.inverse_sum)
                route_step(Router.weights)
                route_step(Router.weights_low)
                weight_part(Q, F, 2)
                run(pooled_low, F)
                mask_experts(M, 6, 7)
                run(weighted_attention, A_)
                mask_experts(M, 7, 8)
                run(weighted_low, A_)

            slots(dve, slot)

        @block.tensor
        def _(pe):
            pe.wait_ge(consts_ready, 1)
            pe.wait_ge(sim_sq_ready, 1)
            for c in range(NC):
                last = pe.matmul(ps_front[:, 0:E], ones[:], sim_sq[:, c, :], start=(c == 0), stop=(c == NC - 1))
            last.then_inc(sim_ss_ready, 1)
            pe.wait_ge(setup_done, 1)

            def transpose_x(F):
                after(pe, pool_split, F.n)
                pe.wait_ge(x_in[F.slot(XR)], 16 * F.turn(XR) + 16)
                for c in range(NC):
                    last = pe.transpose(ps_tall[:, c, :], x_sb[:, F.slot(XR), c * P:(c + 1) * P], ident[:])
                last.then_inc(xT_ready, 1)

            def split_products(psum, pairs, semaphore):
                for i, (left, right) in enumerate(pairs):
                    last = pe.matmul(psum, left, right, start=(i == 0), stop=(i == len(pairs) - 1))
                last.then_inc(semaphore, 1)

            def hidden(F, M):
                after(pe, lg_copied, F.n)
                pe.wait_ge(xT_split, F.n + 1)
                if M is not None:
                    pe.wait_ge(bits_ready, M.n + 1)
                split_products(ps_front[:, 0:S],
                               [(w[:, c, :], t[:, c, :]) for c in range(NC)
                                for w, t in ((W1_hi, xT_hi), (W1_hi, xT_lo), (W1_lo, xT_hi))], h_ready)

            def scores(F):
                pe.wait_ge(tanh_done, F.n + 1)
                pe.matmul(ps_front[:, 0:S], v_wide[:], h_sb[:], start=True, stop=True).then_inc(score_ready, 1)

            def transpose_p1(F):
                pe.wait_ge(p1_ready, F.n + 1)
                pe.transpose(ps_front[:, 0:S], p1[:], ident[:]).then_inc(p1T_ready, 1)

            def pooling(F):
                pe.wait_ge(p1T_copied, F.n + 1)
                for c in range(NC):
                    last = pe.matmul(ps_tall[:, c, :], x_sb[:, F.slot(XR), c * P:(c + 1) * P], p1T[:],
                                     start=True, stop=True)
                last.then_inc(pool_ready, 1)

            def router_products(R):
                pe.wait_ge(pool_split, R.n + 1)
                pe.wait_ge(sq_split, R.n + 1)
                hi = pool_hl[:, R.slot(PR), 0, :].rearrange("p (c s) -> p c s", c=NC)
                lo = pool_hl[:, R.slot(PR), 1, :].rearrange("p (c s) -> p c s", c=NC)
                pairs = [(a[:, c, :], b[:, c, :]) for c in range(NC)
                         for a, b in ((hi, sim_hi), (hi, sim_lo), (lo, sim_hi))]
                for i, (a, b) in enumerate(pairs):
                    pe.matmul(ps_front[:, 0:E], a, b, start=(i == 0), stop=(i == len(pairs) - 1))
                for c in range(NC):
                    pe.matmul(ps_front[:, E:E + 1], sq_hi[:, c, :], ones_bf[:], start=(c == 0), stop=False)
                    last = pe.matmul(ps_front[:, E:E + 1], sq_lo[:, c, :], ones_bf[:], start=False, stop=(c == NC - 1))
                last.then_inc(lg_ready, 1)

            def widen_mask(M, R):
                pe.wait_ge(route_ready, M.n + 1)
                after(pe, ao_e_ready, M.n - (LAG_A - LAG_M))
                for e in range(E):
                    last = pe.matmul(ps_wide[:, e // 4, (e % 4) * S:(e % 4 + 1) * S],
                                     route[:, M.slot(XR), 0, e:e + 1].broadcast_to([P, P]), ident16[:],
                                     start=True, stop=True)
                last.then_inc(mask_ready, 1)
                if R is not None:
                    pe.wait_ge(lg_copied, R.n + 1)
                pe.matmul(ps_front[:, 0:E], ones16[:], route[:, M.slot(XR), 0, :], start=True, stop=True)\
                  .then_inc(counts_ready, 1)

            def widen_weights(A_, M):
                if M is not None:
                    pe.wait_ge(mask_copied, M.n + 1)
                for e in range(E):
                    for h in (1, 2):
                        last = pe.matmul(ps_wide[:, e // 4, (e % 4) * S:(e % 4 + 1) * S],
                                         route[:, A_.slot(XR), h, e:e + 1].broadcast_to([P, P]), ident16[:],
                                         start=(h == 1), stop=(h == 2))
                last.then_inc(weight_wide_ready, 1)

            def load_bits(tile):
                pe.wait_ge(bits_ready, tile.n + 1)
                pe.sem_inc(bits_seen, 1)
                return pe.value_load(active_bits[0:1, tile.slot(XR):tile.slot(XR) + 1])

            def open_bank(psum):
                pe.matmul(psum, zeros16[:, 0:P], zeros16[:, 0:psum.shape[1]],
                          start=True, stop=False)

            def close_bank(psum, semaphore):
                pe.matmul(psum[:, 0:2], zeros16[:, 0:P], zeros16[:, 0:2], start=False, stop=True).then_inc(semaphore, 1)

            def qkv_expert(Q, e, bits):
                pe.wait_ge(pooled_e_ready, Q.n * E + e + 1)
                if isinstance(Q.n, int) and Q.n == 0:
                    pe.wait_ge(w_split, e + 1)
                with pe.If((bits & (1 << e)) != 0):
                    for c in range(NC):
                        hi = pooled_e[:, Q.slot(2), e, 0, c * S:(c + 1) * S]
                        lo = pooled_e[:, Q.slot(2), e, 1, c * S:(c + 1) * S]
                        for a, b in ((hi, w_hi), (hi, w_lo), (lo, w_hi)):
                            pe.matmul(ps_qkv[Q.slot(2)][:, 0:D3], a, b[:, e, c, :], start=False, stop=False)

            def transpose_qk(A_):
                pe.wait_ge(qkv_copied, A_.n + 1)
                pe.transpose(ps_attn[:, 0:S], qkv[:, 0:D], ident[:])
                pe.transpose(ps_attn[:, S:2 * S], qkv[:, D:2 * D], ident[:]).then_inc(qkT_ready, 1)

            def attention_scores(A_):
                pe.wait_ge(qkT_copied, A_.n + 1)
                pe.matmul(ps_attn[:, 0:S], qkT[:, 0, :], qkT[:, 1, :], start=True, stop=True).then_inc(s2_ready, 1)

            def transpose_p2(A_):
                pe.wait_ge(p2_ready, A_.n + 1)
                pe.transpose(ps_attn[:, 0:S], p2[:], ident[:]).then_inc(p2T_ready, 1)

            def attention_output(A_):
                pe.wait_ge(p2T_copied, A_.n + 1)
                pe.matmul(ps_attn[:, 0:S], qkv[:, 2 * D:D3], p2T[:], start=True, stop=True).then_inc(ao_ready, 1)

            def out_expert(O, e, bits):
                hi, lo = ao_hi[:, O.slot(2), e, :], ao_lo[:, O.slot(2), e, :]
                with pe.If((bits & (1 << e)) != 0):
                    for a, b in ((hi, wo_hi), (hi, wo_lo), (lo, wo_hi)):
                        pe.matmul(ps_out[:], a, b[:, e, :], start=False, stop=False)

            def slot(F, R, M, Q, A_, O):
                def q(*experts):
                    for e in experts if Q is not None else ():
                        qkv_expert(Q, e, q_bits)

                def o(*experts):
                    for e in experts if O is not None else ():
                        out_expert(O, e, o_bits)

                def run(step, tile, *more):
                    if tile is not None:
                        step(tile, *more)

                if Q is not None:
                    q_bits = load_bits(Q)
                    open_bank(ps_qkv[Q.slot(2)][:, 0:D3])
                if O is not None:
                    o_bits = load_bits(O)
                run(transpose_x, F)
                run(router_products, R)
                q(0, 1)
                run(widen_mask, M, R)
                if O is not None:
                    pe.wait_ge(ao_split, O.n + 1)
                    after(pe, y_ready, O.n)
                    open_bank(ps_out[:])
                o(0, 1)
                run(hidden, F, M)
                run(transpose_qk, A_)
                q(2)
                o(2)
                run(scores, F)
                run(attention_scores, A_)
                run(widen_weights, A_, M)
                q(3, 4)
                o(3, 4)
                run(transpose_p1, F)
                run(transpose_p2, A_)
                o(5, 6, 7)
                if O is not None:
                    close_bank(ps_out[:], out_ready)
                run(pooling, F)
                run(attention_output, A_)
                q(5, 6, 7)
                if Q is not None:
                    close_bank(ps_qkv[Q.slot(2)][:, 0:D3], qkv_ready)

            slots(pe, slot)


_INS = ['x', 'itok_B_0_2', 'L0_cond_W1', 'L0_cond_b1', 'L0_cond_v', 'L0_ffn_sim_matrix', 'L0_ffn_gates',
        'L0_ffn_q_proj', 'L0_ffn_k_proj', 'L0_ffn_v_proj', 'L0_ffn_o_proj']


def kernel(**inputs):
    import numpy as _np
    import concourse.bacc as _bacc
    from concourse import mybir as _mybir
    from concourse.bass_utils import run_bass_kernel_spmd as _run

    nc = _bacc.Bacc("TRN2", target_bir_lowering=False, num_devices=1)
    arrays, args = {}, []
    for name in _INS:
        a = _np.ascontiguousarray(inputs[name])
        arrays[f"in_{name}_dram"] = a
        args.append(nc.dram_tensor(f"in_{name}_dram", a.shape, _mybir.dt.from_np(a.dtype), kind="ExternalInput").ap())
    shape = inputs['x'].shape
    args.append(nc.dram_tensor("out_0_dram", shape, _mybir.dt.float32, kind="ExternalOutput").ap())
    routed_ffn_kernel(nc, *args)
    r = _run(nc, [arrays], core_ids=[0])
    return r.results[0]["out_0_dram"]
```

```python
import concourse.bass as bass
from concourse import mybir
from contextlib import ExitStack


class Tile:

    RING = 6

    def __init__(self, lap, c):
        self.lap, self.c = lap, c

    def back(self, d):
        return Tile(self.lap, self.c - d)

    @property
    def n(self):
        return self.lap * self.RING + self.c

    def slot(self, ring):
        return self.c % ring

    def turn(self, ring):
        return self.lap * (self.RING // ring) + self.c // ring


def routed_ffn_kernel(nc: bass.Bass, x, itok, W1, b1, v, sim, gates, wq, wk, wv, wo, out):
    fp32, fp16, i32 = mybir.dt.float32, mybir.dt.float16, mybir.dt.int32
    ALU = mybir.AluOpType
    ACT = mybir.ActivationFunctionType
    AX = mybir.AxisListType

    B, S, C = x.shape
    P = 128
    A = W1.shape[1]
    E = sim.shape[1]
    D = wq.shape[2]
    NC = C // P
    D3 = 3 * D
    assert S == P and A == P and D == P
    EPS = 1e-12
    NEG = -1e30
    OFF = 1e9

    SX = 16.0
    SW = 64.0
    SA = 64.0
    ISQ = float(D) ** -0.5

    LAGS = (0, 1, 1, 2, 3, 4)
    LAG_M, LAG_A, LAG_O = LAGS[2], LAGS[4], LAGS[5]
    LOOP_FROM = Tile.RING + LAG_O + (B - LAG_O) % Tile.RING
    LAPS = (B - LOOP_FROM) // Tile.RING
    XR = Tile.RING
    assert XR == LAG_O + 2

    ctx = ExitStack()
    with ctx:
        def sb(name, shape, dt=fp32):
            return ctx.enter_context(nc.sbuf_tensor(name, shape, dt))

        def pb(name, shape, dt=fp32):
            return ctx.enter_context(nc.psum_tensor(name, shape, dt))

        def sem(name):
            return ctx.enter_context(nc.semaphore(name))

        ident = sb("ident", [P, P])
        ident16 = sb("ident16", [P, P], fp16)
        ones = sb("ones", [P, P])
        after_j = sb("after_j", [P, S])
        before_j = sb("before_j", [P, S])
        at_j = sb("at_j", [P, S])
        tie = sb("tie", [P, E, E])
        half = sb("half", [P, 1])
        j_int = sb("j_int", [P, 1], i32)
        counts = sb("counts", [P, 3])
        itok_sb = sb("itok_sb", [P, B], i32)
        NT = 5
        kinds = sb("kinds", [P, B, NT])
        kinds_tmp = sb("kinds_tmp", [P, B])
        W1_raw = sb("W1_raw", [P, NC, A])
        W1_hi = sb("W1_hi", [P, NC, A], fp16)
        W1_lo = sb("W1_lo", [P, NC, A], fp16)
        b1_sb = sb("b1_sb", [P, 1])
        v_sb = sb("v_sb", [P, 1])
        v_wide = sb("v_wide", [P, P])
        sim_sb = sb("sim_sb", [P, NC, E])
        sim_sq = sb("sim_sq", [P, NC, E])
        sim_norm = sb("sim_norm", [P, E])
        sim_hl = sb("sim_hl", [P, NC, 2, E], fp16)
        halves = sb("halves", [P, E])
        bit_e = sb("bit_e", [P, E])
        ones16 = sb("ones16", [P, P], fp16)
        own_block = sb("own_block", [2 * E, E, S], fp16)
        zeros16 = sb("zeros16", [P, P], fp16)
        sig = sb("sig", [P, E])
        WR = 3
        w_raw = sb("w_raw", [P, WR, NC * D3])
        wo_raw = sb("wo_raw", [P, WR, C])
        w_hi = sb("w_hi", [P, E, NC, D3], fp16)
        w_lo = sb("w_lo", [P, E, NC, D3], fp16)
        wo_hi = sb("wo_hi", [P, E, C], fp16)
        wo_lo = sb("wo_lo", [P, E, C], fp16)

        x_sb = sb("x_sb", [P, XR, C])
        kind = sb("kind", [P, XR, NT])
        bias = sb("bias", [P, 2, S])
        bias_tmp = sb("bias_tmp", [P, S])
        xT_hi = sb("xT_hi", [P, NC, S], fp16)
        xT_lo = sb("xT_lo", [P, NC, S], fp16)
        h_sb = sb("h_sb", [P, S])
        s1 = sb("s1", [P, S])
        m1 = sb("m1", [P, 1])
        p1 = sb("p1", [P, S])
        sum1 = sb("sum1", [P, 2])
        p1T = sb("p1T", [P, S])
        PR = 3
        pool_hl = sb("pool_hl", [P, PR, 2, NC * S], fp16)
        pool_sq = sb("pool_sq", [P, NC, S])
        sq_half = sb("sq_half", [P, 2, S])
        sq_sum = sb("sq_sum", [P, S])
        lg = sb("lg", [P, 2 * E + 1])
        lg_sum = sb("lg_sum", [P, E])
        norm = sb("norm", [P, 4])
        logit = sb("logit", [P, E])
        diff = sb("diff", [P, E, E])
        beats = sb("beats", [P, E, E])
        rank = sb("rank", [P, E])
        top2 = sb("top2", [P, E])
        positive = sb("positive", [P, E])
        best = sb("best", [P, 3])
        gated = sb("gated", [P, E])
        masked = sb("masked", [P, E])
        rexp = sb("rexp", [P, E])
        rsum = sb("rsum", [P, 2])
        rw = sb("rw", [P, E])
        route = sb("route", [P, XR, 3, E], fp16)
        active = sb("active", [P, E])
        active_bits = sb("active_bits", [P, XR], i32)
        mask_wide = sb("mask_wide", [P, E, S], fp16)
        pooled_e = sb("pooled_e", [P, 2, E, 2, NC * S], fp16)
        qkv = sb("qkv", [P, D3])
        qkT = sb("qkT", [P, 2, S])
        s2 = sb("s2", [P, S])
        m2 = sb("m2", [P, 1])
        p2 = sb("p2", [P, S])
        sum2 = sb("sum2", [P, 2])
        p2T = sb("p2T", [P, S])
        weightT = sb("weightT", [2 * E, S], fp16)
        weight_blocks = sb("weight_blocks", [2 * E, E, S], fp16)
        aoT = sb("aoT", [P, S])
        ao_e = sb("ao_e", [P, E, S])
        ao_hi = sb("ao_hi", [P, 2, E, S], fp16)
        ao_lo = sb("ao_lo", [P, 2, E, S], fp16)
        y_sb = sb("y_sb", [P, 2, C])

        ps_tall = pb("ps_tall", [P, NC, S])
        ps_front = pb("ps_front", [P, 512])
        ps_attn = pb("ps_attn", [P, 512])
        ps_qkv = [pb(f"ps_qkv{i}", [P, 512]) for i in range(2)]
        ps_out = pb("ps_out", [P, C])
        ps_wide = pb("ps_wide", [P, 2, 512])

        small_in = sem("small_in")
        w_in = [sem(f"w_in{i}") for i in range(WR)]
        consts_ready = sem("consts_ready")
        pool_setup = sem("pool_setup")
        dve_setup = sem("dve_setup")
        sim_sq_ready = sem("sim_sq_ready")
        sim_ss_ready = sem("sim_ss_ready")
        sim_ss_copied = sem("sim_ss_copied")
        sim_norm_ready = sem("sim_norm_ready")
        gate_exp_ready = sem("gate_exp_ready")
        kinds_ready = sem("kinds_ready")
        W1_hi_ready = sem("W1_hi_ready")
        columns_ready = sem("columns_ready")
        w_hi_ready = sem("w_hi_ready")
        w_split = sem("w_split")
        x_in = [sem(f"x_in{i}") for i in range(XR)]
        y_stored = [sem(f"y_stored{i}") for i in range(2)]
        pool_steps = sem("pool_steps")
        bias_ready = sem("bias_ready")
        norm_ready = sem("norm_ready")
        xT_ready = sem("xT_ready")
        xT_hi_ready = sem("xT_hi_ready")
        xT_split = sem("xT_split")
        h_ready = sem("h_ready")
        tanh_done = sem("tanh_done")
        score_ready = sem("score_ready")
        front_steps = sem("front_steps")
        max1_ready = sem("max1_ready")
        exp1_done = sem("exp1_done")
        p1_ready = sem("p1_ready")
        p1T_ready = sem("p1T_ready")
        p1T_copied = sem("p1T_copied")
        pool_ready = sem("pool_ready")
        pool_hi_ready = sem("pool_hi_ready")
        pool_sq_ready = sem("pool_sq_ready")
        sq_halved = sem("sq_halved")
        sq_summed = sem("sq_summed")
        pool_split = sem("pool_split")
        lg_ready = sem("lg_ready")
        lg_copied = sem("lg_copied")
        route_steps = sem("route_steps")
        bit_steps = sem("bit_steps")
        chosen_ready = sem("chosen_ready")
        masked_ready = sem("masked_ready")
        rexp_done = sem("rexp_done")
        route_ready = sem("route_ready")
        mask_ready = sem("mask_ready")
        mask_copied = sem("mask_copied")
        pooled_e_ready = sem("pooled_e_ready")
        counts_ready = sem("counts_ready")
        bits_ready = sem("bits_ready")
        bits_seen = sem("bits_seen")
        qkv_ready = sem("qkv_ready")
        qkv_copied = sem("qkv_copied")
        weightT_copied = sem("weightT_copied")
        blocks_ready = sem("blocks_ready")
        qkT_ready = sem("qkT_ready")
        qkT_copied = sem("qkT_copied")
        s2_ready = sem("s2_ready")
        attn_steps = sem("attn_steps")
        max2_ready = sem("max2_ready")
        exp2_done = sem("exp2_done")
        p2_ready = sem("p2_ready")
        p2T_ready = sem("p2T_ready")
        p2T_copied = sem("p2T_copied")
        weight_wide_ready = sem("weight_wide_ready")
        ao_ready = sem("ao_ready")
        ao_copied = sem("ao_copied")
        ao_e_ready = sem("ao_e_ready")
        ao_hi_ready = sem("ao_hi_ready")
        ao_split = sem("ao_split")
        out_ready = sem("out_ready")
        y_ready = sem("y_ready")

        SMALL_DMAS = 6
        HIGH_DUE = ((2, 0, 1, 1), (1, 0, 0, 1), (1, 1, 0, 0))
        LOW_DUE = ((1, 1, 0, 1), (1, 1, 0, 0), (1, 1, 1, 0))
        assert sum(sum(row) for row in HIGH_DUE) == sum(sum(row) for row in LOW_DUE) == E

        def after(eng, semaphore, value):
            if not isinstance(value, int) or value > 0:
                eng.wait_ge(semaphore, value)

        def due(table, F, part):
            if F is None or not isinstance(F.n, int) or F.n >= len(table):
                return range(0)
            first = sum(sum(row) for row in table[:F.n]) + sum(table[F.n][:part])
            return range(first, first + table[F.n][part])

        def stages(lap, c, peeled):
            tiles = [Tile(lap, c - lag) for lag in LAGS]
            return [None if peeled and not 0 <= t.n < B else t for t in tiles]

        def slots(eng, one_slot, laps=LAPS):
            for c in range(LOOP_FROM):
                one_slot(*stages(0, c, True))
            with eng.Fori(0, laps) as lap:
                for u in range(Tile.RING):
                    one_slot(*stages(lap, LOOP_FROM + u, False))
            for c in range(LOOP_FROM, B + LAG_O - laps * Tile.RING):
                one_slot(*stages(laps, c, True))

        block = ctx.enter_context(nc.Block())

        @block.sync
        def _(sp):
            sp.dma_start(W1_raw[:], W1.rearrange("(c p) a -> p c a", p=P)).then_inc(small_in, 16)
            sp.dma_start(x_sb[:, 0, :], x[0, :, :]).then_inc(x_in[0], 16)
            sp.dma_start(sim_sb[:], sim.rearrange("(c p) e -> p c e", p=P)).then_inc(small_in, 16)
            sp.dma_start(b1_sb[:], b1.rearrange("(a o) -> a o", o=1)).then_inc(small_in, 16)
            sp.dma_start(v_sb[:], v.rearrange("(a o) -> a o", o=1)).then_inc(small_in, 16)
            sp.dma_start(itok_sb[:], itok.rearrange("(o b) -> o b", o=1).broadcast_to([P, B])).then_inc(small_in, 16)
            sp.dma_start(sig[:], gates.rearrange("(o e) -> o e", o=1).broadcast_to([P, E])).then_inc(small_in, 16)

            sp.dma_start(x_sb[:, 1, :], x[1, :, :]).then_inc(x_in[1], 16)
            for e in range(E):
                after(sp, w_split, e - WR + 1)
                raw = w_raw[:, e % WR, :].rearrange("p (c t d) -> p c t d", c=NC, t=3)
                for t, w in enumerate((wq, wk, wv)):
                    sp.dma_start(raw[:, :, t, :], w[e, :, :].rearrange("(c p) d -> p c d", p=P))\
                      .then_inc(w_in[e % WR], 16)
                sp.dma_start(wo_raw[:, e % WR, :], wo[e, :, :]).then_inc(w_in[e % WR], 16)
                if 2 <= e < XR:
                    sp.dma_start(x_sb[:, e, :], x[e, :, :]).then_inc(x_in[e], 16)

            def slot(F, R, M, Q, A_, O):
                ahead = F.back(-1) if F is not None else None
                if ahead is not None and not (isinstance(ahead.n, int) and (ahead.n < XR or ahead.n >= B)):
                    sp.dma_start(x_sb[:, ahead.slot(XR), :],
                                 x[bass.ds(ahead.n, 1), :, :].rearrange("o s c -> (o s) c"))\
                      .then_inc(x_in[ahead.slot(XR)], 16)
                if O is not None:
                    sp.wait_ge(y_ready, O.n + 1)
                    sp.dma_start(out[bass.ds(O.n, 1), :, :].rearrange("o s c -> (o s) c"),
                                 y_sb[:, O.slot(2), :]).then_inc(y_stored[O.slot(2)], 16)

            slots(sp, slot, LAPS - 1)
            for par in range(2):
                sp.wait_ge(y_stored[par], 16 * (B // 2))

        @block.gpsimd
        def _(pool):
            steps = [0]

            def link(ins):
                steps[0] += 1
                ins.then_inc(pool_setup, 1)
                pool.wait_ge(pool_setup, steps[0])

            link(pool.memset(ident[:], 0.0))
            link(pool.affine_select(out=ident[:], in_=ident[:], compare_op=ALU.not_equal, fill=1.0, base=0,
                                    pattern=[[-1, P]], channel_multiplier=1))
            link(pool.tensor_copy(ident16[:], ident[:]))
            link(pool.memset(ones[:], 1.0))
            link(pool.memset(after_j[:], 0.0))
            link(pool.memset(before_j[:], 0.0))
            link(pool.memset(at_j[:], 0.0))
            link(pool.affine_select(out=after_j[:], in_=after_j[:], compare_op=ALU.is_ge, fill=NEG, base=0,
                                    pattern=[[-1, S]], channel_multiplier=1))
            link(pool.affine_select(out=before_j[:], in_=before_j[:], compare_op=ALU.is_ge, fill=NEG, base=0,
                                    pattern=[[1, S]], channel_multiplier=-1))
            link(pool.affine_select(out=at_j[:], in_=at_j[:], compare_op=ALU.not_equal, fill=NEG, base=0,
                                    pattern=[[-1, S]], channel_multiplier=1))
            link(pool.memset(tie[:], 0.0))
            link(pool.affine_select(out=tie[:], in_=tie[:], compare_op=ALU.is_ge, fill=-1e-37, base=0,
                                    pattern=[[-1, E], [1, E]], channel_multiplier=0))
            link(pool.memset(half[:], 0.5))
            link(pool.memset(halves[:], 0.5))
            for e in range(E):
                last = pool.memset(bit_e[:, e:e + 1], float(2 ** e))
            link(last)
            link(pool.memset(ones16[:], 1.0))
            link(pool.memset(zeros16[:], 0.0))
            pool.iota(j_int[:], pattern=[[0, 1]], base=0, channel_multiplier=1).then_inc(consts_ready, 1)
            pool.wait_ge(sim_ss_copied, 1)
            pool.tensor_tensor(out=sim_norm[:], in0=sim_norm[:], in1=halves[:], op=ALU.pow).then_inc(sim_norm_ready, 1)
            link(pool.memset(own_block[:], 0.0))
            for first in (0, E):
                link(pool.affine_select(out=own_block[:], in_=own_block[:], compare_op=ALU.not_equal, fill=1.0,
                                        base=-first, pattern=[[-1, E], [0, S]], channel_multiplier=1))
            pool.wait_ge(kinds_ready, 1)

            BIAS_STEPS = 5

            def norm_of_pooled(R):
                pool.wait_ge(lg_copied, R.n + 1)
                pool.tensor_tensor(out=norm[:, 0:1], in0=lg[:, 2 * E:2 * E + 1], in1=half[:], op=ALU.pow)\
                    .then_inc(norm_ready, 1)

            def type_and_bias(F):
                kcol = kind[:, F.slot(XR), :]
                count = [0]

                def link(ins):
                    count[0] += 1
                    ins.then_inc(pool_steps, 1)
                    pool.wait_ge(pool_steps, F.n * BIAS_STEPS + count[0])

                after(pool, qkv_copied, F.n + 1 - XR)
                link(pool.tensor_copy(kcol, kinds[:, bass.ds(F.n, 1), :].rearrange("p o t -> p (o t)")))
                after(pool, max1_ready, F.n - 1)
                b = bias[:, F.slot(2), :]
                link(pool.tensor_tensor(out=b, in0=after_j[:], in1=kcol[:, 0:1].broadcast_to([P, S]), op=ALU.mult))
                link(pool.tensor_tensor(out=bias_tmp[:], in0=before_j[:], in1=kcol[:, 1:2].broadcast_to([P, S]),
                                        op=ALU.mult))
                link(pool.tensor_tensor(out=b, in0=b, in1=bias_tmp[:], op=ALU.add))
                link(pool.tensor_tensor(out=bias_tmp[:], in0=at_j[:], in1=kcol[:, 2:3].broadcast_to([P, S]),
                                        op=ALU.mult))
                pool.tensor_tensor(out=b, in0=b, in1=bias_tmp[:], op=ALU.add).then_inc(bias_ready, 1)
                assert count[0] == BIAS_STEPS

            def blocks_of_weights(A_):
                pool.wait_ge(weightT_copied, A_.n + 1)
                after(pool, weight_wide_ready, A_.n)
                pool.tensor_tensor(out=weight_blocks[:], in0=own_block[:],
                                   in1=weightT[:].rearrange("r (o s) -> r o s", o=1).broadcast_to([2 * E, E, S]),
                                   op=ALU.mult).then_inc(blocks_ready, 1)

            def sum_of_squares(F):
                pool.wait_ge(pool_sq_ready, F.n + 1)
                pool.tensor_tensor(out=sq_half[:], in0=pool_sq[:, 0:2, :], in1=pool_sq[:, 2:4, :], op=ALU.add)\
                    .then_inc(sq_halved, 1)
                pool.wait_ge(sq_halved, F.n + 1)
                after(pool, lg_ready, F.n)
                pool.tensor_tensor(out=sq_sum[:], in0=sq_half[:, 0, :], in1=sq_half[:, 1, :], op=ALU.add)\
                    .then_inc(sq_summed, 1)

            def slot(F, R, M, Q, A_, O):
                for step, tile in ((norm_of_pooled, R), (type_and_bias, F), (blocks_of_weights, A_),
                                   (sum_of_squares, F)):
                    if tile is not None:
                        step(tile)

            slots(pool, slot)

        @block.scalar
        def _(act):
            act.wait_ge(small_in, 16 * SMALL_DMAS)
            act.activation(W1_hi[:], W1_raw[:], ACT.Copy, scale=SW).then_inc(W1_hi_ready, 1)
            act.activation(sig[:], sig[:], ACT.Exp, scale=-1.0).then_inc(gate_exp_ready, 1)

            def weight_high(e):
                act.wait_ge(w_in[e % WR], 64 * (e // WR + 1))
                act.activation(w_hi[:, e, :, :].rearrange("p c n -> p (c n)"), w_raw[:, e % WR, :], ACT.Copy,
                               scale=SW)
                act.activation(wo_hi[:, e, :], wo_raw[:, e % WR, :], ACT.Copy, scale=SW).then_inc(w_hi_ready, 1)

            def prepare_weights(F, part):
                for e in due(HIGH_DUE, F, part):
                    weight_high(e)

            def slot(F, R, M, Q, A_, O):
                if F is not None:
                    act.wait_ge(xT_ready, F.n + 1)
                    act.activation(xT_hi[:], ps_tall[:], ACT.Copy, scale=SX).then_inc(xT_hi_ready, 1)
                prepare_weights(F, 0)
                if F is not None:
                    act.wait_ge(h_ready, F.n + 1)
                    act.activation(h_sb[:], ps_front[:, 0:S], ACT.Tanh, bias=b1_sb[:], scale=1.0 / (SX * SW))\
                        .then_inc(tanh_done, 1)
                if A_ is not None:
                    act.wait_ge(qkT_ready, A_.n + 1)
                    after(act, blocks_ready, A_.n)
                    act.activation(weightT[:], ps_attn[0:2 * E, 2 * S:3 * S], ACT.Copy).then_inc(weightT_copied, 1)
                    act.activation(qkT[:].rearrange("p t s -> p (t s)"), ps_attn[:, 0:2 * S], ACT.Copy)\
                        .then_inc(qkT_copied, 1)
                if R is not None:
                    act.wait_ge(masked_ready, R.n + 1)
                    act.activation(rexp[:], masked[:], ACT.Exp, bias=best[:, 2:3], accum_out=rsum[:, 0:1])\
                        .then_inc(rexp_done, 1)
                if F is not None:
                    act.wait_ge(max1_ready, F.n + 1)
                    act.activation(p1[:], s1[:], ACT.Exp, bias=m1[:], accum_out=sum1[:, 0:1])\
                        .then_inc(exp1_done, 1)
                if A_ is not None:
                    act.wait_ge(max2_ready, A_.n + 1)
                    act.activation(p2[:], s2[:], ACT.Exp, bias=m2[:], accum_out=sum2[:, 0:1])\
                        .then_inc(exp2_done, 1)
                if M is not None:
                    act.wait_ge(mask_ready, M.n + 1)
                    after(act, pooled_e_ready, M.n * E)
                    act.activation(mask_wide[:].rearrange("p e s -> p (e s)"),
                                   ps_wide[:].rearrange("p h n -> p (h n)"), ACT.Copy).then_inc(mask_copied, 1)
                prepare_weights(F, 1)
                if F is not None:
                    act.wait_ge(p1T_ready, F.n + 1)
                    act.activation(p1T[:], ps_front[:, 0:S], ACT.Copy).then_inc(p1T_copied, 1)
                if A_ is not None:
                    act.wait_ge(p2T_ready, A_.n + 1)
                    act.activation(p2T[:], ps_attn[:, 0:S], ACT.Copy).then_inc(p2T_copied, 1)
                prepare_weights(F, 2)
                if F is not None:
                    act.wait_ge(pool_ready, F.n + 1)
                    after(act, pooled_e_ready, (F.n + 1 - PR) * E)
                    act.activation(pool_hl[:, F.slot(PR), 0, :], ps_tall[:].rearrange("p c s -> p (c s)"), ACT.Copy,
                                   scale=SX).then_inc(pool_hi_ready, 1)
                    after(act, sq_summed, F.n)
                    act.activation(pool_sq[:], ps_tall[:], ACT.Square).then_inc(pool_sq_ready, 1)
                if A_ is not None:
                    act.wait_ge(ao_ready, A_.n + 1)
                    act.activation(aoT[:], ps_attn[:, 0:S], ACT.Copy).then_inc(ao_copied, 1)
                    act.wait_ge(ao_e_ready, A_.n + 1)
                    act.activation(ao_hi[:, A_.slot(2), :, :], ao_e[:], ACT.Copy).then_inc(ao_hi_ready, 1)
                prepare_weights(F, 3)
                if Q is not None:
                    act.wait_ge(qkv_ready, Q.n + 1)
                    act.activation(qkv[:], ps_qkv[Q.slot(2)][:, 0:D3], ACT.Identity, scale=kind[:, Q.slot(XR), 4:5])\
                        .then_inc(qkv_copied, 1)

            slots(act, slot)

        @block.vector
        def _(dve):
            steps = [0]

            def link(ins):
                steps[0] += 1
                ins.then_inc(dve_setup, 1)
                dve.wait_ge(dve_setup, steps[0])

            dve.wait_ge(small_in, 16 * SMALL_DMAS)
            dve.tensor_tensor(out=sim_sq[:], in0=sim_sb[:], in1=sim_sb[:], op=ALU.mult).then_inc(sim_sq_ready, 1)
            dve.wait_ge(W1_hi_ready, 1)
            dve.scalar_tensor_tensor(out=W1_lo[:], in0=W1_raw[:], scalar=SW, in1=W1_hi[:], op0=ALU.mult,
                                     op1=ALU.subtract)
            dve.wait_ge(consts_ready, 1)
            dve.tensor_scalar(v_wide[:], ones[:], v_sb[:], None, ALU.mult)
            link(dve.tensor_copy(counts[:, 0:1], j_int[:]))
            link(dve.tensor_scalar(counts[:, 1:2], counts[:, 0:1], -1.0, float(S), ALU.mult, ALU.add))
            link(dve.tensor_scalar(counts[:, 0:1], counts[:, 0:1], 1.0, None, ALU.add))
            link(dve.memset(counts[:, 2:3], float(S - 1)))
            link(dve.reciprocal(counts[:], counts[:]))
            link(dve.tensor_copy(kinds_tmp[:], itok_sb[:]))
            link(dve.tensor_scalar(kinds[:, :, 0], kinds_tmp[:], 0.0, None, ALU.is_equal))
            link(dve.tensor_scalar(kinds[:, :, 1], kinds_tmp[:], 1.0, None, ALU.is_equal))
            link(dve.tensor_tensor(out=kinds[:, :, 2], in0=kinds[:, :, 0], in1=kinds[:, :, 1], op=ALU.add))
            link(dve.tensor_scalar(kinds[:, :, 2], kinds[:, :, 2], -1.0, 1.0, ALU.mult, ALU.add))
            link(dve.tensor_scalar(kinds[:, :, 3], kinds[:, :, 0], counts[:, 0:1], None, ALU.mult))
            link(dve.scalar_tensor_tensor(out=kinds_tmp[:], in0=kinds[:, :, 1], scalar=counts[:, 1:2],
                                          in1=kinds[:, :, 3], op0=ALU.mult, op1=ALU.add))
            link(dve.scalar_tensor_tensor(out=kinds[:, :, 3], in0=kinds[:, :, 2], scalar=counts[:, 2:3],
                                          in1=kinds_tmp[:], op0=ALU.mult, op1=ALU.add))
            dve.tensor_scalar(kinds[:, :, 4], kinds[:, :, 3], 1.0 / (SX * SW), None, ALU.mult)\
               .then_inc(kinds_ready, 1)
            dve.wait_ge(sim_ss_ready, 1)
            dve.tensor_copy(sim_norm[:], ps_front[:, 0:E]).then_inc(sim_ss_copied, 1)

            def router_columns():
                dve.wait_ge(sim_norm_ready, 1)
                link(dve.tensor_scalar(sim_norm[:], sim_norm[:], EPS, None, ALU.max))
                link(dve.reciprocal(sim_norm[:], sim_norm[:]))
                for c in range(NC):
                    last = dve.tensor_tensor(out=sim_sb[:, c, :], in0=sim_sb[:, c, :], in1=sim_norm[:], op=ALU.mult)
                link(last)
                link(dve.tensor_scalar(sim_sb[:], sim_sb[:], SW, None, ALU.mult))
                link(dve.tensor_copy(sim_hl[:, :, 0, :], sim_sb[:]))
                link(dve.tensor_tensor(out=sim_hl[:, :, 1, :], in0=sim_sb[:], in1=sim_hl[:, :, 0, :], op=ALU.subtract))
                dve.wait_ge(gate_exp_ready, 1)
                link(dve.tensor_scalar(sig[:], sig[:], 1.0, None, ALU.add))
                dve.reciprocal(sig[:], sig[:]).then_inc(columns_ready, 1)

            def weight_low(e):
                dve.wait_ge(w_hi_ready, e + 1)
                dve.scalar_tensor_tensor(out=w_lo[:, e, :, :].rearrange("p c n -> p (c n)"),
                                         in0=w_raw[:, e % WR, :], scalar=SW,
                                         in1=w_hi[:, e, :, :].rearrange("p c n -> p (c n)"),
                                         op0=ALU.mult, op1=ALU.subtract)
                dve.scalar_tensor_tensor(out=wo_lo[:, e, :], in0=wo_raw[:, e % WR, :], scalar=SW,
                                         in1=wo_hi[:, e, :], op0=ALU.mult, op1=ALU.subtract).then_inc(w_split, 1)

            def prepare_weights(F, part):
                for e in due(LOW_DUE, F, part):
                    weight_low(e)

            FRONT_STEPS, ATTN_STEPS, BIT_STEPS, ROUTE_STEPS = 2, 2, 1, 11

            class Steps:

                def __init__(self, semaphore, tile, per_tile):
                    self.semaphore, self.tile, self.per_tile, self.count = semaphore, tile, per_tile, 0

                def mark(self, ins):
                    self.count += 1
                    assert self.count <= self.per_tile
                    ins.then_inc(self.semaphore, 1)

                def wait(self):
                    dve.wait_ge(self.semaphore, self.tile.n * self.per_tile + self.count)

            def mask_experts(M, first, end):
                if M is None:
                    return
                for e in range(first, end):
                    if e == 0:
                        dve.wait_ge(mask_copied, M.n + 1)
                        after(dve, qkv_ready, M.n - 1)
                    dve.tensor_tensor(
                        out=pooled_e[:, M.slot(2), e, :, :].rearrange("p h (c s) -> p (h c) s", s=S),
                        in0=pool_hl[:, M.slot(PR), :, :].rearrange("p h (c s) -> p (h c) s", s=S),
                        in1=mask_wide[:, e:e + 1, :].broadcast_to([P, 2 * NC, S]),
                        op=ALU.mult).then_inc(pooled_e_ready, 1)

            def expert_bits(M):
                if M is None:
                    return
                steps = Steps(bit_steps, M, BIT_STEPS)
                dve.wait_ge(counts_ready, M.n + 1)
                steps.mark(dve.scalar_tensor_tensor(out=active[:], in0=ps_front[:, 0:E], scalar=0.5, in1=bit_e[:],
                                                    op0=ALU.is_gt, op1=ALU.mult))
                steps.wait()
                with nc.allow_low_precision("small integers"):
                    dve.tensor_reduce(out=active_bits[:, M.slot(XR):M.slot(XR) + 1], in_=active[:], axis=AX.X,
                                      op=ALU.add).then_inc(bits_ready, 1)

            def xT_low(F):
                dve.wait_ge(xT_hi_ready, F.n + 1)
                dve.scalar_tensor_tensor(out=xT_lo[:], in0=ps_tall[:], scalar=SX, in1=xT_hi[:],
                                         op0=ALU.mult, op1=ALU.subtract).then_inc(xT_split, 1)

            def masked_scores(F, A_):
                if F is not None:
                    front = Steps(front_steps, F, FRONT_STEPS)
                    dve.wait_ge(score_ready, F.n + 1)
                    dve.wait_ge(bias_ready, F.n + 1)
                    front.mark(dve.tensor_tensor(out=s1[:], in0=ps_front[:, 0:S], in1=bias[:, F.slot(2), :],
                                                 op=ALU.add))
                if A_ is not None:
                    attn = Steps(attn_steps, A_, ATTN_STEPS)
                    dve.wait_ge(s2_ready, A_.n + 1)
                    attn.mark(dve.scalar_tensor_tensor(out=s2[:], in0=ps_attn[:, 0:S], scalar=ISQ, in1=after_j[:],
                                                       op0=ALU.mult, op1=ALU.add))
                if F is not None:
                    front.wait()
                    dve.tensor_reduce(out=m1[:], in_=s1[:], axis=AX.X, op=ALU.max, negate=True)\
                       .then_inc(max1_ready, 1)
                if A_ is not None:
                    attn.wait()
                    dve.tensor_reduce(out=m2[:], in_=s2[:], axis=AX.X, op=ALU.max, negate=True)\
                       .then_inc(max2_ready, 1)

            def normalise(F, A_):
                if F is not None:
                    front = Steps(front_steps, F, FRONT_STEPS)
                    front.count = 1
                    dve.wait_ge(exp1_done, F.n + 1)
                    front.mark(dve.reciprocal(sum1[:, 1:2], sum1[:, 0:1]))
                if A_ is not None:
                    attn = Steps(attn_steps, A_, ATTN_STEPS)
                    attn.count = 1
                    dve.wait_ge(exp2_done, A_.n + 1)
                    attn.mark(dve.reciprocal(sum2[:, 1:2], sum2[:, 0:1]))
                if F is not None:
                    front.wait()
                    dve.tensor_scalar(p1[:], p1[:], sum1[:, 1:2], None, ALU.mult).then_inc(p1_ready, 1)
                if A_ is not None:
                    attn.wait()
                    dve.tensor_scalar(p2[:], p2[:], sum2[:, 1:2], None, ALU.mult).then_inc(p2_ready, 1)

            def pooled_low(F):
                dve.wait_ge(pool_sq_ready, F.n + 1)
                dve.scalar_tensor_tensor(out=pool_hl[:, F.slot(PR), 1, :],
                                         in0=ps_tall[:].rearrange("p c s -> p (c s)"), scalar=SX,
                                         in1=pool_hl[:, F.slot(PR), 0, :], op0=ALU.mult, op1=ALU.subtract)\
                   .then_inc(pool_split, 1)

            def weighted_attention(A_):
                dve.wait_ge(weight_wide_ready, A_.n + 1)
                dve.wait_ge(ao_copied, A_.n + 1)
                dve.tensor_tensor(out=ao_e[:], in0=ps_wide[:].rearrange("p h (e s) -> p (h e) s", s=S),
                                  in1=aoT[:].rearrange("p (o s) -> p o s", o=1).broadcast_to([P, E, S]),
                                  op=ALU.mult).then_inc(ao_e_ready, 1)

            def weighted_low(A_):
                dve.wait_ge(ao_hi_ready, A_.n + 1)
                dve.tensor_tensor(out=ao_lo[:, A_.slot(2), :, :], in0=ao_e[:], in1=ao_hi[:, A_.slot(2), :, :],
                                  op=ALU.subtract).then_inc(ao_split, 1)

            def add_x(O):
                dve.wait_ge(out_ready, O.n + 1)
                after(dve, y_stored[O.slot(2)], 16 * O.turn(2))
                dve.scalar_tensor_tensor(out=y_sb[:, O.slot(2), :], in0=ps_out[:], scalar=1.0 / (SA * SW),
                                         in1=x_sb[:, O.slot(XR), :], op0=ALU.mult, op1=ALU.add)\
                   .then_inc(y_ready, 1)

            class Router:

                def __init__(self, R):
                    self.R = R
                    self.steps = Steps(route_steps, R, ROUTE_STEPS)
                    self.mask, self.w_hi, self.w_lo = (route[:, R.slot(XR), i, :] for i in range(3))

                def take_products(self):
                    dve.wait_ge(lg_ready, self.R.n + 1)
                    dve.tensor_copy(lg[:], ps_front[:, 0:2 * E + 1]).then_inc(lg_copied, 1)

                def guarded_norm(self):
                    dve.wait_ge(norm_ready, self.R.n + 1)
                    self.steps.mark(dve.tensor_scalar(norm[:, 1:2], norm[:, 0:1], kind[:, self.R.slot(XR), 3:4], EPS,
                                                      ALU.mult, ALU.max))

                def inverse_norm(self):
                    self.steps.wait()
                    self.steps.mark(dve.reciprocal(norm[:, 2:3], norm[:, 1:2]))

                def join_parts(self):
                    dve.tensor_tensor(out=lg_sum[:], in0=lg[:, 0:E], in1=lg[:, E:2 * E], op=ALU.add)

                def logit_scale(self):
                    self.steps.wait()
                    self.steps.mark(dve.tensor_scalar(norm[:, 3:4], norm[:, 2:3], kind[:, self.R.slot(XR), 4:5], None,
                                                      ALU.mult))

                def logits(self):
                    self.steps.wait()
                    self.steps.mark(dve.scalar_tensor_tensor(out=logit[:], in0=lg_sum[:], scalar=norm[:, 3:4],
                                                             in1=sig[:], op0=ALU.mult, op1=ALU.subtract))

                def differences(self):
                    self.steps.wait()
                    dve.tensor_tensor(out=diff[:],
                                      in0=logit[:].rearrange("p (o e) -> p o e", o=1).broadcast_to([P, E, E]),
                                      in1=logit[:].rearrange("p (e o) -> p e o", o=1).broadcast_to([P, E, E]),
                                      op=ALU.subtract)
                    dve.tensor_scalar(positive[:], logit[:], 0.0, None, ALU.is_gt)
                    self.steps.mark(dve.tensor_reduce(out=best[:, 0:1], in_=logit[:], axis=AX.X, op=ALU.max))

                def comparisons(self):
                    self.steps.wait()
                    dve.tensor_tensor(out=beats[:], in0=diff[:], in1=tie[:], op=ALU.is_gt)
                    dve.tensor_scalar(best[:, 2:3], best[:, 0:1], -1.0, 0.0, ALU.mult, ALU.min)
                    self.steps.mark(dve.tensor_scalar(best[:, 1:2], best[:, 0:1], 0.0, None, ALU.is_le))

                def ranks(self):
                    self.steps.wait()
                    self.steps.mark(dve.tensor_reduce(out=rank[:], in_=beats[:], axis=AX.X, op=ALU.add))

                def two_best(self):
                    self.steps.wait()
                    self.steps.mark(dve.tensor_scalar(top2[:], rank[:], 2.0, best[:, 1:2], ALU.is_lt, ALU.mult))

                def set_mask(self):
                    self.steps.wait()
                    dve.tensor_tensor(out=self.mask, in0=top2[:], in1=positive[:], op=ALU.max)\
                       .then_inc(chosen_ready, 1)

                def gate(self):
                    dve.wait_ge(chosen_ready, self.R.n + 1)
                    dve.scalar_tensor_tensor(out=gated[:], in0=logit[:], scalar=0.0, in1=self.mask,
                                             op0=ALU.max, op1=ALU.mult)
                    self.steps.mark(dve.tensor_scalar(masked[:], self.mask, -1.0, OFF, ALU.add, ALU.mult))

                def masked_logits(self):
                    self.steps.wait()
                    dve.tensor_tensor(out=masked[:], in0=masked[:], in1=gated[:], op=ALU.add)\
                       .then_inc(masked_ready, 1)

                def inverse_sum(self):
                    dve.wait_ge(rexp_done, self.R.n + 1)
                    self.steps.mark(dve.reciprocal(rsum[:, 1:2], rsum[:, 0:1]))

                def weights(self):
                    self.steps.wait()
                    dve.tensor_scalar(rw[:], rexp[:], rsum[:, 1:2], SA, ALU.mult, ALU.mult)
                    self.steps.mark(dve.tensor_scalar(self.w_hi, rexp[:], rsum[:, 1:2], SA, ALU.mult, ALU.mult))

                def weights_low(self):
                    self.steps.wait()
                    dve.tensor_tensor(out=self.w_lo, in0=rw[:], in1=self.w_hi, op=ALU.subtract)\
                       .then_inc(route_ready, 1)
                    assert self.steps.count == ROUTE_STEPS

            def slot(F, R, M, Q, A_, O):
                def run(step, tile):
                    if tile is not None:
                        step(tile)

                router = Router(R) if R is not None else None

                def route_step(step):
                    if router is not None:
                        step(router)

                run(xT_low, F)
                route_step(Router.take_products)
                prepare_weights(F, 0)
                if F is not None and R is None:
                    router_columns()
                mask_experts(Q, 6, 7)
                route_step(Router.guarded_norm)
                for step in (Router.inverse_norm, Router.join_parts, Router.logit_scale, Router.logits,
                             Router.differences, Router.comparisons, Router.ranks, Router.two_best,
                             Router.set_mask, Router.gate, Router.masked_logits):
                    route_step(step)
                mask_experts(Q, 7, 8)
                masked_scores(F, A_)
                route_step(Router.inverse_sum)
                normalise(F, A_)
                route_step(Router.weights)
                prepare_weights(F, 1)
                prepare_weights(F, 2)
                mask_experts(M, 0, 1)
                route_step(Router.weights_low)
                mask_experts(M, 1, 6)
                prepare_weights(F, 3)
                run(pooled_low, F)
                run(expert_bits, M)
                run(weighted_attention, A_)
                run(add_x, O)
                run(weighted_low, A_)

            slots(dve, slot)

        @block.tensor
        def _(pe):
            pe.wait_ge(consts_ready, 1)
            pe.wait_ge(sim_sq_ready, 1)
            for c in range(NC):
                last = pe.matmul(ps_front[:, 0:E], ones[:], sim_sq[:, c, :], start=(c == 0), stop=(c == NC - 1))
            last.then_inc(sim_ss_ready, 1)
            pe.wait_ge(sim_ss_copied, 1)

            def transpose_x(F):
                after(pe, pool_split, F.n)
                pe.wait_ge(x_in[F.slot(XR)], 16 * F.turn(XR) + 16)
                for c in range(NC):
                    last = pe.transpose(ps_tall[:, c, :], x_sb[:, F.slot(XR), c * P:(c + 1) * P], ident[:])
                last.then_inc(xT_ready, 1)

            def split_products(psum, pairs, semaphore):
                for i, (left, right) in enumerate(pairs):
                    last = pe.matmul(psum, left, right, start=(i == 0), stop=(i == len(pairs) - 1))
                last.then_inc(semaphore, 1)

            def hidden(F):
                after(pe, lg_copied, F.n)
                pe.wait_ge(xT_split, F.n + 1)
                split_products(ps_front[:, 0:S],
                               [(w[:, c, :], t[:, c, :]) for c in range(NC)
                                for w, t in ((W1_hi, xT_hi), (W1_hi, xT_lo), (W1_lo, xT_hi))], h_ready)

            def scores(F):
                pe.wait_ge(tanh_done, F.n + 1)
                pe.matmul(ps_front[:, 0:S], v_wide[:], h_sb[:], start=True, stop=True).then_inc(score_ready, 1)

            def transpose_p1(F):
                pe.wait_ge(p1_ready, F.n + 1)
                pe.transpose(ps_front[:, 0:S], p1[:], ident[:]).then_inc(p1T_ready, 1)

            def pooling(F):
                pe.wait_ge(p1T_copied, F.n + 1)
                for c in range(NC):
                    last = pe.matmul(ps_tall[:, c, :], x_sb[:, F.slot(XR), c * P:(c + 1) * P], p1T[:],
                                     start=True, stop=True)
                last.then_inc(pool_ready, 1)

            def sum_of_squares(R):
                pe.wait_ge(sq_summed, R.n + 1)
                after(pe, bits_ready, R.n)
                pe.matmul(ps_front[:, 2 * E:2 * E + 1], sq_sum[:], ones[:, 0:1], start=True, stop=True)

            def router_products(R):
                pe.wait_ge(pool_split, R.n + 1)
                if isinstance(R.n, int) and R.n == 0:
                    pe.wait_ge(columns_ready, 1)
                hi = pool_hl[:, R.slot(PR), 0, :].rearrange("p (c s) -> p c s", c=NC)
                lo = pool_hl[:, R.slot(PR), 1, :].rearrange("p (c s) -> p c s", c=NC)
                for c in range(NC):
                    pe.matmul(ps_front[:, 0:2 * E], hi[:, c, :], sim_hl[:, c, :, :].rearrange("p h e -> p (h e)"),
                              start=(c == 0), stop=False)
                    last = pe.matmul(ps_front[:, 0:E], lo[:, c, :], sim_hl[:, c, 0, :], start=False, stop=(c == NC - 1))
                last.then_inc(lg_ready, 1)

            def widen_mask(M):
                pe.wait_ge(chosen_ready, M.n + 1)
                after(pe, ao_e_ready, M.n - (LAG_A - LAG_M))
                for e in range(E):
                    last = pe.matmul(ps_wide[:, e // 4, (e % 4) * S:(e % 4 + 1) * S],
                                     route[:, M.slot(XR), 0, e:e + 1].broadcast_to([P, P]), ident16[:],
                                     start=True, stop=True)
                last.then_inc(mask_ready, 1)

            def count_tokens(M, F):
                if F is not None:
                    pe.wait_ge(p1T_copied, F.n + 1)
                pe.matmul(ps_front[:, 0:E], ones16[:], route[:, M.slot(XR), 0, :], start=True, stop=True)\
                  .then_inc(counts_ready, 1)

            def widen_weights(A_, M):
                pe.wait_ge(blocks_ready, A_.n + 1)
                if M is not None:
                    pe.wait_ge(mask_copied, M.n + 1)
                for h in range(2):
                    last = pe.matmul(ps_wide[:, h, :], ones16[0:2 * E, :],
                                     weight_blocks[:, h * E // 2:(h + 1) * E // 2, :].rearrange("r e s -> r (e s)"),
                                     start=True, stop=True)
                last.then_inc(weight_wide_ready, 1)

            def load_bits(tile):
                pe.wait_ge(bits_ready, tile.n + 1)
                pe.sem_inc(bits_seen, 1)
                return pe.value_load(active_bits[0:1, tile.slot(XR):tile.slot(XR) + 1])

            def close_bank(psum, semaphore):
                pe.matmul(psum[:, 0:2], zeros16[:, 0:P], zeros16[:, 0:2], start=False, stop=True).then_inc(semaphore, 1)

            def sum_products(psum, products, e, bits):
                if e == 0:
                    pe.matmul(psum, *products[0], start=True, stop=False)
                    products = products[1:]
                with pe.If((bits & (1 << e)) != 0):
                    for a, b in products:
                        pe.matmul(psum, a, b, start=False, stop=False)

            def qkv_expert(Q, e, bits):
                pe.wait_ge(pooled_e_ready, Q.n * E + e + 1)
                if isinstance(Q.n, int) and Q.n == 0:
                    pe.wait_ge(w_split, e + 1)
                products = []
                for c in range(NC):
                    hi = pooled_e[:, Q.slot(2), e, 0, c * S:(c + 1) * S]
                    lo = pooled_e[:, Q.slot(2), e, 1, c * S:(c + 1) * S]
                    products += [(a, b[:, e, c, :]) for a, b in ((hi, w_hi), (hi, w_lo), (lo, w_hi))]
                sum_products(ps_qkv[Q.slot(2)][:, 0:D3], products, e, bits)

            def transpose_qk(A_):
                pe.wait_ge(route_ready, A_.n + 1)
                pe.matmul(ps_attn[0:2 * E, 2 * S:3 * S],
                          route[:, A_.slot(XR), 1:3, :].rearrange("p h e -> p (h e)"), ident16[:],
                          start=True, stop=True)
                pe.wait_ge(qkv_copied, A_.n + 1)
                pe.transpose(ps_attn[:, 0:S], qkv[:, 0:D], ident[:])
                pe.transpose(ps_attn[:, S:2 * S], qkv[:, D:2 * D], ident[:]).then_inc(qkT_ready, 1)

            def attention_scores(A_):
                pe.wait_ge(qkT_copied, A_.n + 1)
                pe.matmul(ps_attn[:, 0:S], qkT[:, 0, :], qkT[:, 1, :], start=True, stop=True).then_inc(s2_ready, 1)

            def transpose_p2(A_):
                pe.wait_ge(p2_ready, A_.n + 1)
                pe.transpose(ps_attn[:, 0:S], p2[:], ident[:]).then_inc(p2T_ready, 1)

            def attention_output(A_):
                pe.wait_ge(p2T_copied, A_.n + 1)
                pe.matmul(ps_attn[:, 0:S], qkv[:, 2 * D:D3], p2T[:], start=True, stop=True).then_inc(ao_ready, 1)

            def out_expert(O, e, bits):
                if e == 0:
                    pe.wait_ge(ao_split, O.n + 1)
                    after(pe, y_ready, O.n)
                hi, lo = ao_hi[:, O.slot(2), e, :], ao_lo[:, O.slot(2), e, :]
                sum_products(ps_out[:], [(a, b[:, e, :]) for a, b in ((hi, wo_hi), (hi, wo_lo), (lo, wo_hi))],
                             e, bits)

            def slot(F, R, M, Q, A_, O):
                def q(*experts):
                    for e in experts if Q is not None else ():
                        qkv_expert(Q, e, q_bits)

                def o(*experts):
                    for e in experts if O is not None else ():
                        out_expert(O, e, o_bits)

                def run(step, tile, *more):
                    if tile is not None:
                        step(tile, *more)

                if O is not None:
                    o_bits = load_bits(O)
                run(transpose_x, F)
                run(sum_of_squares, R)
                if Q is not None:
                    q_bits = load_bits(Q)
                run(router_products, R)
                q(0, 1)
                o(0)
                run(hidden, F)
                run(transpose_qk, A_)
                o(1, 2)
                q(2)
                run(scores, F)
                run(attention_scores, A_)
                q(3)
                o(3)
                run(widen_mask, M)
                q(4, 5)
                o(4)
                run(transpose_p1, F)
                run(transpose_p2, A_)
                run(widen_weights, A_, M)
                o(5)
                run(pooling, F)
                run(attention_output, A_)
                run(count_tokens, M, F)
                o(6, 7)
                if O is not None:
                    close_bank(ps_out[:], out_ready)
                q(6, 7)
                if Q is not None:
                    close_bank(ps_qkv[Q.slot(2)][:, 0:D3], qkv_ready)

            slots(pe, slot)


_INS = ['x', 'itok_B_0_2', 'L0_cond_W1', 'L0_cond_b1', 'L0_cond_v', 'L0_ffn_sim_matrix', 'L0_ffn_gates',
        'L0_ffn_q_proj', 'L0_ffn_k_proj', 'L0_ffn_v_proj', 'L0_ffn_o_proj']


def kernel(**inputs):
    import numpy as _np
    import concourse.bacc as _bacc
    from concourse import mybir as _mybir
    from concourse.bass_utils import run_bass_kernel_spmd as _run

    nc = _bacc.Bacc("TRN2", target_bir_lowering=False, num_devices=1)
    arrays, args = {}, []
    for name in _INS:
        a = _np.ascontiguousarray(inputs[name])
        arrays[f"in_{name}_dram"] = a
        args.append(nc.dram_tensor(f"in_{name}_dram", a.shape, _mybir.dt.from_np(a.dtype), kind="ExternalInput").ap())
    shape = inputs['x'].shape
    args.append(nc.dram_tensor("out_0_dram", shape, _mybir.dt.float32, kind="ExternalOutput").ap())
    routed_ffn_kernel(nc, *args)
    r = _run(nc, [arrays], core_ids=[0])
    return r.results[0]["out_0_dram"]
```
